# Optimizing a Trainium2 kernel written in Bass

```python
import numpy as np
import jax
import jax.numpy as jnp

def _softmax(x, axis=-1):
    return jax.nn.softmax(x, axis=axis)

def _gelu(x):
    return jax.nn.gelu(x, approximate=True)

def _silu(x):
    return jax.nn.silu(x)

def _sigmoid(x):
    return jax.nn.sigmoid(x)

def _layernorm(x, axis=-1, eps=1e-05):
    m = jnp.mean(x, axis=axis, keepdims=True)
    v = jnp.var(x, axis=axis, keepdims=True)
    return (x - m) / jnp.sqrt(v + eps)

def _scatter_add(tgt, idx, src, axis=0):
    return tgt.at[idx].add(src)

def _segment_sum(src, seg, n):
    return jax.ops.segment_sum(src, seg, n)
kernel_name = 'mk_seq_preln_d1_jaxref_r4_33fa9e'

def setup_inputs(seed: int=0):
    np.random.seed(seed)
    _w = jnp.asarray

    def _L0_attn_setup():
        import jax, jax.numpy as jnp
        import numpy as np
        NUM_HEADS = 4
        CHUNK = 64
        GATE_NORM = 16.0
        EPS = 1e-05

        def _xavier(key, fan_in, fan_out):
            gain = 2.0 ** (-2.5)
            limit = gain * np.sqrt(6.0 / (fan_in + fan_out))
            return jax.random.uniform(key, (fan_in, fan_out), jnp.float32, -limit, limit)

        def _to_chunks(t, B, H, NC, C):
            d = t.shape[-1]
            return t.reshape(B, H, NC, C, d).transpose(2, 0, 1, 3, 4)

        def _gla_forward(x, Wq, Wk, Wv, Wg, gk_w1, gk_w2, gk_b2, g_norm_w, Wo):
            B, L, D = x.shape
            H = NUM_HEADS
            C = CHUNK
            NC = L // C
            q = x @ Wq
            k = x @ Wk
            v = x @ Wv
            gk = jax.nn.log_sigmoid(x @ gk_w1 @ gk_w2 + gk_b2) / GATE_NORM

            def split_heads(t):
                return t.reshape(B, L, H, -1).transpose(0, 2, 1, 3)
            q, k, v, gk = map(split_heads, (q, k, v, gk))
            dk = q.shape[-1]
            scale = dk ** (-0.5)
            qc = _to_chunks(q, B, H, NC, C)
            kc = _to_chunks(k, B, H, NC, C)
            vc = _to_chunks(v, B, H, NC, C)
            gc = _to_chunks(gk, B, H, NC, C)
            Bcum = jnp.cumsum(gc, axis=3)
            causal = jnp.tril(jnp.ones((C, C), jnp.float32))

            def step(Hst, inp):
                qi, ki, vi, bi = inp
                qg = qi * jnp.exp(bi) * scale
                kg = ki * jnp.exp(-bi)
                o_inter = jnp.einsum('bhcd,bhde->bhce', qg, Hst)
                A = jnp.einsum('bhtd,bhsd->bhts', qg, kg) * causal
                o_intra = jnp.einsum('bhts,bhse->bhte', A, vi)
                b_last = bi[:, :, -1:, :]
                kH = ki * jnp.exp(b_last - bi)
                H_new = jnp.exp(b_last).transpose(0, 1, 3, 2) * Hst + jnp.einsum('bhcd,bhce->bhde', kH, vi)
                return (H_new, o_inter + o_intra)
            dv = v.shape[-1]
            H0 = jnp.zeros((B, H, dk, dv), jnp.float32)
            _, oc = jax.lax.scan(step, H0, (qc, kc, vc, Bcum))
            o = oc.transpose(1, 2, 0, 3, 4).reshape(B, H, L, dv)
            o = o.transpose(0, 2, 1, 3)
            rms = jnp.sqrt(jnp.mean(o * o, axis=-1, keepdims=True) + EPS)
            o_n = o / rms * g_norm_w
            g = (x @ Wg).reshape(B, L, H, dv)
            o = o_n * g * jax.nn.sigmoid(g)
            return o.reshape(B, L, H * dv) @ Wo
        key = jax.random.key(seed)
        ks = jax.random.split(key, 8)
        B, L, D = (4, 512, 256)
        Dk, Dv, R = (256, 512, 16)
        x = jax.random.normal(ks[0], (B, L, D), jnp.float32)
        return {'x': x, 'Wq': _xavier(ks[1], D, Dk), 'Wk': _xavier(ks[2], D, Dk), 'Wv': _xavier(ks[3], D, Dv), 'Wg': _xavier(ks[4], D, Dv), 'gk_w1': _xavier(ks[5], D, R), 'gk_w2': _xavier(ks[6], R, Dk), 'gk_b2': jnp.zeros((Dk,), jnp.float32), 'g_norm_w': jnp.ones((Dv // NUM_HEADS,), jnp.float32), 'Wo': _xavier(ks[7], Dv, D)}
    _L0_attn_in = _L0_attn_setup()

    def _L0_ffn_setup():
        import jax, jax.numpy as jnp
        import numpy as np
        D_MODEL, D_FF, RANK = (256, 1024, 64)
        B, S = (4, 1024)
        key = jax.random.key(seed)
        ks = jax.random.split(key, 7)
        return {'x': jax.random.normal(ks[0], (B, S, D_MODEL), dtype=jnp.float32), 'U1': jax.random.normal(ks[1], (D_MODEL, RANK), dtype=jnp.float32) * 0.02, 'V1': jax.random.normal(ks[2], (RANK, D_FF), dtype=jnp.float32) * 0.02, 'b1': jnp.zeros((D_FF,), dtype=jnp.float32), 'U2': jax.random.normal(ks[3], (D_FF, RANK), dtype=jnp.float32) * 0.02, 'V2': jax.random.normal(ks[4], (RANK, D_MODEL), dtype=jnp.float32) * 0.02, 'b2': jnp.zeros((D_MODEL,), dtype=jnp.float32)}
    _L0_ffn_in = _L0_ffn_setup()
    _d = {'L0_attn_x': _L0_attn_in['x'], 'L0_attn_Wq': _L0_attn_in['Wq'], 'L0_attn_Wk': _L0_attn_in['Wk'], 'L0_attn_Wv': _L0_attn_in['Wv'], 'L0_attn_Wg': _L0_attn_in['Wg'], 'L0_attn_gk_w1': _L0_attn_in['gk_w1'], 'L0_attn_gk_w2': _L0_attn_in['gk_w2'], 'L0_attn_gk_b2': _L0_attn_in['gk_b2'], 'L0_attn_g_norm_w': _L0_attn_in['g_norm_w'], 'L0_attn_Wo': _L0_attn_in['Wo'], 'L0_ffn_U1': _L0_ffn_in['U1'], 'L0_ffn_V1': _L0_ffn_in['V1'], 'L0_ffn_b1': _L0_ffn_in['b1'], 'L0_ffn_U2': _L0_ffn_in['U2'], 'L0_ffn_V2': _L0_ffn_in['V2'], 'L0_ffn_b2': _L0_ffn_in['b2']}
    _x0 = _d['L0_attn_x']
    _d['L0_attn_x'] = jax.random.normal(jax.random.fold_in(jax.random.key(seed), 1), (4, 1024, 256), dtype=_x0.dtype)
    del _x0
    return _d

def reference(L0_attn_x, L0_attn_Wq, L0_attn_Wk, L0_attn_Wv, L0_attn_Wg, L0_attn_gk_w1, L0_attn_gk_w2, L0_attn_gk_b2, L0_attn_g_norm_w, L0_attn_Wo, L0_ffn_U1, L0_ffn_V1, L0_ffn_b1, L0_ffn_U2, L0_ffn_V2, L0_ffn_b2):

    def _L0_attn_ref(x, Wq, Wk, Wv, Wg, gk_w1, gk_w2, gk_b2, g_norm_w, Wo):
        import jax, jax.numpy as jnp
        import numpy as np
        NUM_HEADS = 4
        CHUNK = 64
        GATE_NORM = 16.0
        EPS = 1e-05

        def _xavier(key, fan_in, fan_out):
            gain = 2.0 ** (-2.5)
            limit = gain * np.sqrt(6.0 / (fan_in + fan_out))
            return jax.random.uniform(key, (fan_in, fan_out), jnp.float32, -limit, limit)

        def _to_chunks(t, B, H, NC, C):
            d = t.shape[-1]
            return t.reshape(B, H, NC, C, d).transpose(2, 0, 1, 3, 4)

        def _gla_forward(x, Wq, Wk, Wv, Wg, gk_w1, gk_w2, gk_b2, g_norm_w, Wo):
            B, L, D = x.shape
            H = NUM_HEADS
            C = CHUNK
            NC = L // C
            q = x @ Wq
            k = x @ Wk
            v = x @ Wv
            gk = jax.nn.log_sigmoid(x @ gk_w1 @ gk_w2 + gk_b2) / GATE_NORM

            def split_heads(t):
                return t.reshape(B, L, H, -1).transpose(0, 2, 1, 3)
            q, k, v, gk = map(split_heads, (q, k, v, gk))
            dk = q.shape[-1]
            scale = dk ** (-0.5)
            qc = _to_chunks(q, B, H, NC, C)
            kc = _to_chunks(k, B, H, NC, C)
            vc = _to_chunks(v, B, H, NC, C)
            gc = _to_chunks(gk, B, H, NC, C)
            Bcum = jnp.cumsum(gc, axis=3)
            causal = jnp.tril(jnp.ones((C, C), jnp.float32))

            def step(Hst, inp):
                qi, ki, vi, bi = inp
                qg = qi * jnp.exp(bi) * scale
                kg = ki * jnp.exp(-bi)
                o_inter = jnp.einsum('bhcd,bhde->bhce', qg, Hst)
                A = jnp.einsum('bhtd,bhsd->bhts', qg, kg) * causal
                o_intra = jnp.einsum('bhts,bhse->bhte', A, vi)
                b_last = bi[:, :, -1:, :]
                kH = ki * jnp.exp(b_last - bi)
                H_new = jnp.exp(b_last).transpose(0, 1, 3, 2) * Hst + jnp.einsum('bhcd,bhce->bhde', kH, vi)
                return (H_new, o_inter + o_intra)
            dv = v.shape[-1]
            H0 = jnp.zeros((B, H, dk, dv), jnp.float32)
            _, oc = jax.lax.scan(step, H0, (qc, kc, vc, Bcum))
            o = oc.transpose(1, 2, 0, 3, 4).reshape(B, H, L, dv)
            o = o.transpose(0, 2, 1, 3)
            rms = jnp.sqrt(jnp.mean(o * o, axis=-1, keepdims=True) + EPS)
            o_n = o / rms * g_norm_w
            g = (x @ Wg).reshape(B, L, H, dv)
            o = o_n * g * jax.nn.sigmoid(g)
            return o.reshape(B, L, H * dv) @ Wo
        return _gla_forward(x, Wq, Wk, Wv, Wg, gk_w1, gk_w2, gk_b2, g_norm_w, Wo)

    def _L0_ffn_ref(x, U1, V1, b1, U2, V2, b2):
        import jax, jax.numpy as jnp
        import numpy as np
        D_MODEL, D_FF, RANK = (256, 1024, 64)
        B, S = (4, 1024)
        P = jnp.einsum('bsd,dr->bsr', x, U1)
        H = jax.nn.gelu(jnp.einsum('bsr,rf->bsf', P, V1) + b1)
        Q = jnp.einsum('bsf,fr->bsr', H, U2)
        return jnp.einsum('bsr,rd->bsd', Q, V2) + b2
    x = L0_attn_x
    x = x + _L0_attn_ref(_layernorm(x, axis=-1), L0_attn_Wq, L0_attn_Wk, L0_attn_Wv, L0_attn_Wg, L0_attn_gk_w1, L0_attn_gk_w2, L0_attn_gk_b2, L0_attn_g_norm_w, L0_attn_Wo)
    x = x + _L0_ffn_ref(_layernorm(x, axis=-1), L0_ffn_U1, L0_ffn_V1, L0_ffn_b1, L0_ffn_U2, L0_ffn_V2, L0_ffn_b2)
    return x

_drawn_inputs = setup_inputs


def setup_inputs(seed=0):
    import zlib

    import numpy as np

    out = dict(_drawn_inputs(seed))
    spreads = {'L0_attn_gk_b2': (0.0, 0.8),
     'L0_attn_g_norm_w': (1.0, 0.6),
     'L0_ffn_b1': (0.0, 0.8),
     'L0_ffn_b2': (0.0, 0.8)}
    factors = {'L0_attn_Wq': 3.814,
     'L0_attn_Wk': 3.784,
     'L0_attn_Wv': 3.803,
     'L0_attn_Wg': 3.805,
     'L0_attn_gk_w1': 8.0,
     'L0_attn_gk_w2': 8.0,
     'L0_attn_Wo': 3.799,
     'L0_ffn_U1': 8.0,
     'L0_ffn_V1': 8.0,
     'L0_ffn_U2': 8.0,
     'L0_ffn_V2': 8.0}
    for name, (base, spread) in spreads.items():
        noise = np.random.default_rng([zlib.crc32(name.encode()), seed]).standard_normal(out[name].shape)
        drawn = base * np.exp(spread * noise) if base else spread * noise
        out[name] = jnp.asarray(drawn.astype(out[name].dtype))
    for name, factor in factors.items():
        out[name] = (out[name] * factor).astype(out[name].dtype)
    return out
```

```python
from contextlib import ExitStack

import concourse.bass as bass
from concourse import mybir

ALU = mybir.AluOpType
ACT = mybir.ActivationFunctionType
AX_X = mybir.AxisListType.X
F32 = mybir.dt.float32
F32R = mybir.dt.float32r

P = 128
ALL = slice(None)
CHUNK = 64
HEADS = 4
GATE_NORM = 16.0
EPS = 1e-5


def count_past(eng, sem, n):
    if not isinstance(n, int) or n > 0:
        eng.wait_ge(sem, n)


def build(nc, x, Wq, Wk, Wv, Wg, gk_w1, gk_w2, gk_b2, g_norm_w, Wo, U1, V1, b1, U2, V2, b2, out):
    B, L, D = x.shape
    DK = Wq.shape[1]
    DV = Wv.shape[1]
    R = gk_w1.shape[1]
    dk, dv = DK // HEADS, DV // HEADS
    RF, FF = V1.shape
    KC = D // P
    MC = DK // P
    FC = FF // P
    PAIRS = B // 2
    STEPS = PAIRS * L // P
    TOK = 2 * P
    SCALE = float(dk) ** -0.5
    assert (KC, MC, dv, dk, FC, PAIRS) == (2, 2, 128, 64, 8, 2)

    with ExitStack() as ctx:
        def sb(name, *shape):
            return ctx.enter_context(nc.sbuf_tensor(name, list(shape), F32))

        def sem(name):
            return ctx.enter_context(nc.semaphore(name))

        banks = [ctx.enter_context(nc.psum_tensor(f"bank{i}", [P, 512], F32)) for i in range(8)]

        def parts(name, *shape):
            return [ctx.enter_context(nc.sbuf_tensor(f"{name}_{x}", list(shape), F32R)) for x in ("hi", "lo")]

        wq, wk = sb("wq", P, KC, DK), sb("wk", P, KC, DK)
        wv, wg = sb("wv", P, KC, DV), sb("wg", P, KC, DV)
        w1, w2 = sb("w1", P, KC, 2, R), sb("w2", 4 * R, DK)
        wo = sb("wo", P, HEADS, D)
        u1, v1 = sb("u1", P, KC, 2, RF), sb("v1", P, FF)
        u2, v2 = sb("u2", P, FC, RF), sb("v2", P, D)
        wq_p, wk_p = parts("wq", P, KC, DK), parts("wk", P, KC, DK)
        wv_p, wg_p = parts("wv", P, KC, DV), parts("wg", P, KC, DV)
        wo_p, v1_p, u1_p = parts("wo", P, HEADS, D), parts("v1", P, FF), parts("u1", P, KC, 2 * RF)
        w2_p, v2_p = parts("w2", 4 * R, DK), parts("v2", P, D)
        w1_s = ctx.enter_context(nc.sbuf_tensor("w1_s", [P, KC, 2, 2, R], F32R))
        u2_s = ctx.enter_context(nc.sbuf_tensor("u2_s", [P, FC, 2, RF], F32R))
        gate_bias = sb("gate_bias", P, MC)
        norm_w = sb("norm_w", P, 1)
        ff_bias = sb("ff_bias", P, FC)
        out_bias = sb("out_bias", P, D)
        ident = sb("ident", P, P)
        causal = sb("causal", P, P)
        carry = sb("carry", P, MC * TOK)
        neg_half, eps, eps_sum = sb("neg_half", P, 8), sb("eps", P, 2), sb("eps_sum", P, 8)

        x_n = [sb(f"x_n{c}", P, 2, D) for c in range(2)]
        x_res = [sb(f"x_res{c}", P, 2, D) for c in range(2)]
        stats1, mv1, rstd1 = sb("stats1", P, 2, 6), sb("mv1", P, 2, 2), sb("rstd1", P, 2)
        var1 = sb("var1", P, 2)
        spare = sb("spare", P, 1)
        xn = sb("xn", P, 2, D)
        xnT = parts("xnT", P, KC, TOK)
        lowT = ctx.enter_context(nc.sbuf_tensor("lowT", [4 * R, TOK], F32R))
        absz, expz, log1 = sb("absz", P, MC, TOK), sb("expz", P, MC * TOK), sb("log1", P, MC * TOK)
        minz = sb("minz", P, MC, TOK)
        logsig, decay = sb("logsig", P, MC * TOK), sb("decay", P, MC * TOK)
        eb, enb = sb("eb", P, MC * TOK), sb("enb", P, MC * TOK)
        qg, kg = sb("qg", P, MC * TOK), sb("kg", P, MC * TOK)
        qs, kh = sb("qs", P, MC * TOK), sb("kh", P, MC * TOK)
        k0 = sb("k0", P, MC * 2, CHUNK)
        e01 = sb("e01", P, MC * 2)
        kht = sb("kht", P, 2, DK)
        vals = sb("vals", P, 2, DV)
        tanh_g, gate = sb("tanh_g", P, 2, DV), sb("gate", P, 2, DV)
        probs = sb("probs", P, 2, HEADS, P)
        state = [sb(f"state{c}", P, MC, 2, dv) for c in range(2)]
        sq, ssq = sb("sq", P, 2, HEADS * dv), sb("ssq", P, 2 * HEADS)
        meansq, rrms = sb("meansq", P, 2 * HEADS), sb("rrms", P, 2 * HEADS)
        y = sb("y", P, 2, DV)
        yT = parts("yT", P, 2, HEADS, P)
        x2 = [sb(f"x2_{c}", P, 2, D) for c in range(2)]
        x2b = sb("x2b", P, 2, D)
        stats2, mv2, rstd2 = sb("stats2", P, 2, 6), sb("mv2", P, 2, 2), sb("rstd2", P, 2)
        var2 = sb("var2", P, 2)
        x2n = sb("x2n", P, 2, D)
        x2nT = parts("x2nT", P, KC, TOK)
        pT = ctx.enter_context(nc.sbuf_tensor("pT", [P, TOK], F32R))
        hT, hT_p = sb("hT", P, FC, TOK), parts("hT", P, FC, TOK)
        qT = parts("qT", P, TOK)
        res = sb("res", P, 2, D)

        def by_chunk(t):
            return t[:, :].rearrange("p (g c s) -> p g c s", c=2, s=CHUNK)

        def by_tile(t):
            return t[:, :].rearrange("p (m j s) -> p m j s", m=MC, j=2)

        ebc, kgc, qgc, qsc, khc = (by_chunk(t) for t in (eb, kg, qg, qs, kh))
        qgt, kgt, qst, kht_in = (by_tile(t) for t in (qg, kg, qs, kh))
        last = CHUNK - 1

        def over_chunk(col):
            return col.to_broadcast([P, MC * 2, CHUNK])

        consts = sem("consts")
        wo_scaled = sem("wo_scaled")
        names = ("w1", "w2", "zb", "wv", "wq", "wk", "wg", "nw", "wo", "u1", "v1", "u2", "v2", "fb", "b2")
        in_of = {n: sem(f"in_{n}") for n in names}
        hi_of = {n: sem(f"hi_{n}") for n in ("w1", "w2", "wv", "wq", "wk", "wg", "wo", "u1", "v1", "u2", "v2")}
        split_of = {n: sem(f"split_{n}") for n in hi_of}
        x_in = [sem(f"x_in{c}") for c in range(2)]
        xres_in = [sem(f"xres_in{c}") for c in range(2)]
        stats1_done, mv1_done, var1_done, rstd1_done, xn_done = map(
            sem, ("stats1_done", "mv1_done", "var1_done", "rstd1_done", "xn_done"))
        xnT_ps, xnT_hi, xnT_done = sem("xnT_ps"), sem("xnT_hi"), sem("xnT_done")
        low_ps, low_hi, low_done = sem("low_ps"), sem("low_hi"), sem("low_done")
        z_ps, absz_done, expz_done, log1_done = map(sem, ("z_ps", "absz_done", "expz_done", "log1_done"))
        minz_done, logsig_done, decay_done = map(sem, ("minz_done", "logsig_done", "decay_done"))
        eb_done, enb_done = sem("eb_done"), sem("enb_done")
        v_ps, v_done = [sem(f"v_ps{j}") for j in range(2)], [sem(f"v_done{j}") for j in range(2)]
        q_ps, k_ps, qg_done, kg_done = map(sem, ("q_ps", "k_ps", "qg_done", "kg_done"))
        k0_done, kh_done, qs0_done, qs1_done, e01_done = map(
            sem, ("k0_done", "kh_done", "qs0_done", "qs1_done", "e01_done"))
        g_ps, tanh_done, gate_done = ([sem(f"{n}{j}") for j in range(2)] for n in ("g_ps", "tanh_done", "gate_done"))
        score_ps, probs_done = ([sem(f"{n}{j}") for j in range(2)] for n in ("score_ps", "probs_done"))
        kht_ps, kht_done = sem("kht_ps"), sem("kht_done")
        o_ps, sq_done, ssq_done, y_done = ([sem(f"{n}{j}") for j in range(2)] for n in ("o_ps", "sq_done", "ssq_done", "y_done"))
        state_ps, state_done = sem("state_ps"), sem("state_done")
        meansq_done, rrms_done = sem("meansq_done"), sem("rrms_done")
        yT_ps, yT_hi, yT_done = ([sem(f"{n}{j}") for j in range(2)] for n in ("yT_ps", "yT_hi", "yT_done"))
        proj_ps, x2_done, x2b_done = sem("proj_ps"), sem("x2_done"), sem("x2b_done")
        stats2_done, mv2_done, var2_done, rstd2_done, x2n_done = map(
            sem, ("stats2_done", "mv2_done", "var2_done", "rstd2_done", "x2n_done"))
        x2nT_ps, x2nT_hi, x2nT_done, pT_ps, pT_hi, pT_done = map(
            sem, ("x2nT_ps", "x2nT_hi", "x2nT_done", "pT_ps", "pT_hi", "pT_done"))
        h_ps, gelu_done, h_hi, h_lo = ([sem(f"{n}{b}") for b in range(4)] for n in ("h_ps", "gelu_done", "h_hi", "h_lo"))
        qT_ps, qT_hi, qT_done, ff_ps, res_done, stored = map(sem, ("qT_ps", "qT_hi", "qT_done", "ff_ps", "res_done", "stored"))

        x_dram = x.rearrange("(c j) (i p) d -> c i p j d", c=PAIRS, p=P)
        out_dram = out.rearrange("(c j) (i p) d -> c i p j d", c=PAIRS, p=P)

        def rows(w, n):
            return w.rearrange("(k p) n -> p k n", k=n)

        loads = [
            ("w1", w1[:, :, 0, :], rows(gk_w1, KC)), ("w1", w1[:, :, 1, :], rows(gk_w1, KC)),
            *(("w2", w2[r * R:(r + 1) * R, :], gk_w2) for r in range(4)),
            ("zb", gate_bias[:, :], gk_b2),
            ("wv", wv[:, :, :], rows(Wv, KC)), ("wq", wq[:, :, :], rows(Wq, KC)), ("wk", wk[:, :, :], rows(Wk, KC)),
            ("wg", wg[:, :, :], rows(Wg, KC)),
            ("nw", norm_w[:, :], g_norm_w.rearrange("(p a) -> p a", a=1)),
            ("wo", wo[:, :, :], rows(Wo, HEADS)),
            ("u1", u1[:, :, 0, :], rows(U1, KC)), ("u1", u1[:, :, 1, :], rows(U1, KC)),
            ("v1", v1[0:RF, :], V1), ("v1", v1[RF:P, :], V1),
            ("u2", u2[:, :, :], rows(U2, FC)),
            ("v2", v2[0:RF, :], V2), ("v2", v2[RF:P, :], V2),
            ("fb", ff_bias[:, :], b1),
            ("b2", out_bias[:, :], b2.rearrange("(a d) -> a d", a=1).to_broadcast([P, D])),
        ]

        def arrived(eng, name):
            eng.wait_ge(in_of[name], 16 * sum(n == name for n, _, _ in loads))

        flat = {
            "w1": (w1[:, :, :, :], w1_s[:, :, :, 0, :], w1_s[:, :, :, 1, :]),
            "w2": (w2[:, :], w2_p[0][:, :], w2_p[1][:, :]),
            "wv": (wv[:, :, :], wv_p[0][:, :, :], wv_p[1][:, :, :]),
            "wq": (wq[:, :, :], wq_p[0][:, :, :], wq_p[1][:, :, :]),
            "wk": (wk[:, :, :], wk_p[0][:, :, :], wk_p[1][:, :, :]),
            "wg": (wg[:, :, :], wg_p[0][:, :, :], wg_p[1][:, :, :]),
            "wo": (wo[:, :, :], wo_p[0][:, :, :], wo_p[1][:, :, :]),
            "u1": (u1[:, :, :, :].rearrange("p k a r -> p k (a r)"), u1_p[0][:, :, :], u1_p[1][:, :, :]),
            "v1": (v1[:, :], v1_p[0][:, :], v1_p[1][:, :]),
            "u2": (u2[:, :, :], u2_s[:, :, 0, :], u2_s[:, :, 1, :]),
            "v2": (v2[:, :], v2_p[0][:, :], v2_p[1][:, :]),
        }

        def weight_hi(act, name):
            arrived(act, name)
            if name == "wo":
                act.wait_ge(wo_scaled, 1)
            act.activation(flat[name][1], flat[name][0], ACT.Copy).then_inc(hi_of[name], 1)

        def weight_lo(eng, name):
            eng.wait_ge(hi_of[name], 1)
            eng.tensor_tensor(flat[name][2], flat[name][0], flat[name][1].bitcast(F32), ALU.subtract).then_inc(split_of[name], 1)

        N_CONSTS = 11

        def on(step):
            return not isinstance(step, int) or 0 <= step < STEPS

        def v_order(step):
            return (0, 1) if isinstance(step, int) and step == 0 else (1, 0)

        def run(eng, slot, before=None):
            for t in range(-2, 2):
                if before is not None:
                    before(t)
                slot(t, t // 2, t % 2)
            with eng.Fori(1, STEPS // 2 - 1) as i:
                for c in range(2):
                    slot(2 * i + c, i, c)
            for t in range(STEPS - 2, STEPS + 1):
                slot(t, t // 2, t % 2)

        block = ctx.enter_context(nc.Block())

        @block.sync
        def _(sp):
            def before(t):
                for name, dst, src in {-1: loads[:5], 0: loads[5:]}.get(t, ()):
                    sp.dma_start(dst, src).then_inc(in_of[name], 16)

            def load_x(s, i, c):
                count_past(sp, xn_done, s - 1)
                sp.dma_start(x_n[c][:, :, :], x_dram[c, i]).then_inc(x_in[c], 16)

            def slot(t, i, c):
                if on(t + 2):
                    load_x(t + 2, i + 1, c)
                if on(t):
                    count_past(sp, x2_done, t - 1)
                    sp.dma_start(x_res[c][:, :, :], x_dram[c, i]).then_inc(xres_in[c], 16)
                if on(t - 1):
                    j = i - 1 + c
                    sp.wait_ge(res_done, t)
                    sp.dma_start(out_dram[1 - c, j], res[:, :, :]).then_inc(stored, 16)

            run(sp, slot, before)
            sp.wait_ge(stored, 16 * STEPS)

        @block.gpsimd
        def _(pool):
            pool.memset(neg_half[:, :], -0.5).then_inc(consts, 1)
            pool.memset(eps[:, :], EPS).then_inc(consts, 1)
            pool.memset(eps_sum[:, :], EPS * dv).then_inc(consts, 1)
            pool.memset(ident[:, :], 0.0).then_inc(consts, 1)
            pool.memset(causal[:, :], 1.0).then_inc(consts, 1)
            pool.wait_ge(consts, 8)
            pool.affine_select(out=ident[:, :], in_=ident[:, :], compare_op=ALU.not_equal, fill=1.0,
                               base=0, pattern=[[-1, P]], channel_multiplier=1).then_inc(consts, 1)
            pool.affine_select(out=causal[:, :], in_=causal[:, :], compare_op=ALU.is_ge, fill=0.0,
                               base=0, pattern=[[1, P]], channel_multiplier=-1).then_inc(consts, 1)

            def before(t):
                for name in {-1: ("w1", "w2"), 0: ("wo", "u1", "v1", "u2", "v2")}.get(t, ()):
                    weight_lo(pool, name)

            def slot(t, i, c):
                a, p, f, n = t, t + 1, t - 1, t + 2
                if on(n):
                    pool.wait_ge(mv1_done, n + 1)
                    pool.tensor_tensor(var1[:, :], mv1[:, :, 1], eps[:, 0:2], ALU.add).then_inc(var1_done, 1)
                    pool.wait_ge(var1_done, n + 1)
                    pool.tensor_tensor(rstd1[:, :], var1[:, :], neg_half[:, 0:2], ALU.pow).then_inc(rstd1_done, 1)
                if on(a):
                    for j in range(2):
                        pool.wait_ge(ssq_done[j], a + 1)
                    pool.tensor_tensor(meansq[:, :], ssq[:, :], eps_sum[:, :], ALU.add).then_inc(meansq_done, 1)
                    pool.wait_ge(meansq_done, a + 1)
                    pool.tensor_tensor(rrms[:, :], meansq[:, :], neg_half[:, :], ALU.pow).then_inc(rrms_done, 1)
                if on(f):
                    for b in range(4):
                        fc = slice(2 * b, 2 * b + 2)
                        pool.wait_ge(h_hi[b], f + 1)
                        pool.tensor_tensor(hT_p[1][:, fc, :], hT[:, fc, :], hT_p[0][:, fc, :].bitcast(F32), ALU.subtract).then_inc(h_lo[b], 1)
                if on(p):
                    if isinstance(p, int) and p == 0:
                        weight_lo(pool, "wk")
                        weight_lo(pool, "wg")
                    pool.wait_ge(eb_done, p + 1)
                    count_past(pool, state_done, p)
                    pool.tensor_tensor(e01[:, :], ebc[:, :, 0, last], ebc[:, :, 1, last], ALU.mult).then_inc(e01_done, 1)
                    pool.wait_ge(qg_done, p + 1)
                    pool.tensor_tensor(qsc[:, :, 1, :], qgc[:, :, 1, :], over_chunk(ebc[:, :, 0, last:]), ALU.mult).then_inc(qs1_done, 1)
                    pool.wait_ge(kg_done, p + 1)
                    pool.tensor_tensor(k0[:, :, :], kgc[:, :, 0, :], over_chunk(ebc[:, :, 0, last:]), ALU.mult).then_inc(k0_done, 1)
                    pool.tensor_tensor(khc[:, :, 1, :], kgc[:, :, 1, :], over_chunk(ebc[:, :, 1, last:]), ALU.mult)
                    pool.wait_ge(k0_done, p + 1)
                    pool.tensor_tensor(khc[:, :, 0, :], k0[:, :, :], over_chunk(ebc[:, :, 1, last:]), ALU.mult).then_inc(kh_done, 1)
                if on(a):
                    pool.wait_ge(mv2_done, a + 1)
                    pool.tensor_tensor(var2[:, :], mv2[:, :, 1], eps[:, 0:2], ALU.add).then_inc(var2_done, 1)
                    pool.wait_ge(var2_done, a + 1)
                    pool.tensor_tensor(rstd2[:, :], var2[:, :], neg_half[:, 0:2], ALU.pow).then_inc(rstd2_done, 1)
                    count_past(pool, res_done, a)
                    if isinstance(a, int) and a == 0:
                        arrived(pool, "b2")
                    pool.tensor_tensor(x2b[:, :, :], x2[c][:, :, :], out_bias[:, :].unsqueeze(1).to_broadcast([P, 2, D]), ALU.add).then_inc(x2b_done, 1)

            run(pool, slot, before)

        @block.scalar
        def _(act):
            def before(t):
                for name in {-1: ("w1", "w2"), 0: ("wo", "u1", "v1", "u2", "v2")}.get(t, ()):
                    weight_hi(act, name)

            def slot(t, i, c):
                a, p, f = t, t + 1, t - 1
                if on(p):
                    act.wait_ge(xnT_ps, p + 1)
                    act.activation(xnT[0][:, :, :].rearrange("p k s -> p (k s)"), banks[5][:, :], ACT.Copy).then_inc(xnT_hi, 1)
                    if isinstance(p, int) and p == 0:
                        for name in ("wv", "wq", "wk"):
                            weight_hi(act, name)
                if on(a):
                    act.wait_ge(kht_ps, a + 1)
                    act.activation(kht[:, :, :].rearrange("p j d -> p (j d)"), banks[2][:, :], ACT.Copy).then_inc(kht_done, 1)
                if on(f):
                    act.wait_ge(x2nT_ps, f + 1)
                    act.activation(x2nT[0][:, :, :].rearrange("p k s -> p (k s)"), banks[3][:, :], ACT.Copy).then_inc(x2nT_hi, 1)
                if on(p):
                    if isinstance(p, int) and p == 0:
                        arrived(act, "zb")
                    act.preload_act_table_set("natural_log_exp_and_others")
                    act.wait_ge(z_ps, p + 1)
                    for m in range(MC):
                        zabs = act.activation(absz[:, m, :], banks[3][:, m * TOK:(m + 1) * TOK], ACT.Abs, bias=gate_bias[:, m:m + 1])
                    zabs.then_inc(absz_done, 1)
                    act.wait_ge(absz_done, p + 1)
                    act.activation(expz[:, :], absz[:, :, :].rearrange("p m s -> p (m s)"), ACT.Exp, scale=-1.0).then_inc(expz_done, 1)
                    act.wait_ge(expz_done, p + 1)
                    act.activation(log1[:, :], expz[:, :], ACT.Ln, bias=1.0).then_inc(log1_done, 1)
                    if isinstance(p, int) and p == 0:
                        weight_hi(act, "wg")
                if on(a):
                    for j in range(2):
                        act.wait_ge(o_ps[j], a + 1)
                        for h in range(HEADS):
                            e = slice(h * dv, (h + 1) * dv)
                            sq_sum = act.activation(sq[:, j, e], banks[j][:, e], ACT.Square, accum_out=ssq[:, j * HEADS + h:j * HEADS + h + 1])
                        sq_sum.then_inc(ssq_done[j], 1)
                if on(p):
                    act.wait_ge(decay_done, p + 1)
                    act.activation(eb[:, :], decay[:, :], ACT.Exp, scale=1.0 / GATE_NORM).then_inc(eb_done, 1)
                    act.activation(enb[:, :], decay[:, :], ACT.Exp, scale=-1.0 / GATE_NORM).then_inc(enb_done, 1)
                if on(f):
                    if isinstance(f, int) and f == 0:
                        arrived(act, "fb")
                    for b in range(4):
                        act.wait_ge(h_ps[b], f + 1)
                        for k in range(2):
                            fc = 2 * b + k
                            g = act.activation(hT[:, fc, :], banks[4 + b][:, k * TOK:(k + 1) * TOK], ACT.Gelu_apprx_tanh, bias=ff_bias[:, fc:fc + 1])
                        g.then_inc(gelu_done[b], 1)
                if on(p):
                    for j in v_order(p):
                        act.wait_ge(v_ps[j], p + 1)
                        act.activation(vals[:, j, :], banks[2 + j][:, :], ACT.Copy).then_inc(v_done[j], 1)
                if on(a):
                    for j in range(2):
                        act.wait_ge(yT_ps[j], a + 1)
                        act.activation(yT[0][:, j, :, :].rearrange("p h s -> p (h s)"), banks[6 + j][:, :], ACT.Copy).then_inc(yT_hi[j], 1)
                if on(p):
                    for j in range(2):
                        act.wait_ge(g_ps[j], p + 1)
                        act.activation(tanh_g[:, j, :], banks[j][:, :], ACT.Tanh, scale=0.5).then_inc(tanh_done[j], 1)

            run(act, slot, before)

        @block.vector
        def _(dve):
            dve.memset(carry[:, :], 1.0).then_inc(consts, 1)
            dve.memset(state[0][:, :, :, :], 0.0).then_inc(consts, 1)
            dve.memset(state[1][:, :, :, :], 0.0).then_inc(consts, 1)
            dve.wait_ge(consts, 8)
            dve.memset(carry[:, :].rearrange("p (g s) -> p g s", s=CHUNK)[:, :, 0:1], 0.0).then_inc(consts, 1)
            dve.wait_ge(consts, N_CONSTS)

            def before(t):
                if t == 0:
                    arrived(dve, "nw")
                    arrived(dve, "wo")
                    dve.tensor_scalar(wo[:, :, :], wo[:, :, :], norm_w[:, 0:1], 0.5 * float(dv) ** 0.5, ALU.mult, ALU.mult).then_inc(wo_scaled, 1)

            def slot(t, i, c):
                a, p, f, n = t, t + 1, t - 1, t + 2
                if on(p):
                    dve.wait_ge(xnT_hi, p + 1)
                    dve.tensor_tensor(xnT[1][:, :, :].rearrange("p k s -> p (k s)"), banks[5][:, :],
                                      xnT[0][:, :, :].rearrange("p k s -> p (k s)").bitcast(F32), ALU.subtract).then_inc(xnT_done, 1)
                if on(f):
                    dve.wait_ge(rstd2_done, f + 1)
                    for j in range(2):
                        xj = dve.tensor_scalar(x2n[:, j, :], x2[1 - c][:, j, :], mv2[:, j, 0:1], rstd2[:, j:j + 1], ALU.subtract, ALU.mult)
                    xj.then_inc(x2n_done, 1)
                if on(a):
                    for hh in range(2):
                        dve.wait_ge(score_ps[hh], a + 1)
                        dve.tensor_tensor(probs[:, hh, :, :], banks[hh][:, :].rearrange("p (g s) -> p g s", g=4),
                                          causal[:, :].unsqueeze(1).to_broadcast([P, 4, P]), ALU.mult).then_inc(probs_done[hh], 1)
                if on(p):
                    if isinstance(p, int) and p == 0:
                        weight_lo(dve, "wv")
                    dve.wait_ge(low_ps, p + 1)
                    dve.tensor_copy(lowT[:, :], banks[6][0:4 * R, 0:TOK]).then_inc(low_hi, 1)
                    dve.wait_ge(low_hi, p + 1)
                    dve.tensor_tensor(lowT[2 * R:4 * R, :], banks[6][2 * R:4 * R, 0:TOK], lowT[2 * R:4 * R, :].bitcast(F32), ALU.subtract).then_inc(low_done, 1)
                if on(f):
                    dve.wait_ge(x2nT_hi, f + 1)
                    dve.tensor_tensor(x2nT[1][:, :, :].rearrange("p k s -> p (k s)"), banks[3][:, :],
                                      x2nT[0][:, :, :].rearrange("p k s -> p (k s)").bitcast(F32), ALU.subtract).then_inc(x2nT_done, 1)
                if on(n):
                    dve.wait_ge(x_in[c], 16 * (i + 2))
                    for j in range(2):
                        st = dve.bn_stats(stats1[:, j, :], x_n[c][:, j, :])
                    st.then_inc(stats1_done, 1)
                    dve.wait_ge(stats1_done, n + 1)
                    dve.tensor_copy(spare[:, :], stats1[:, 1, 0:1])
                    for j in range(2):
                        st = dve.bn_aggr(mv1[:, j, :], stats1[:, j, :])
                    st.then_inc(mv1_done, 1)
                if on(p):
                    if isinstance(p, int) and p == 0:
                        weight_lo(dve, "wq")
                    dve.wait_ge(absz_done, p + 1)
                    for m in range(MC):
                        mz = dve.tensor_scalar(minz[:, m, :], banks[3][:, m * TOK:(m + 1) * TOK], gate_bias[:, m:m + 1], 0.0, ALU.add, ALU.min)
                    mz.then_inc(minz_done, 1)
                if on(f):
                    dve.wait_ge(pT_ps, f + 1)
                    dve.tensor_copy(pT[:, :], banks[4][:, 0:TOK]).then_inc(pT_hi, 1)
                    dve.wait_ge(pT_hi, f + 1)
                    dve.tensor_tensor(pT[RF:P, :], banks[4][RF:P, 0:TOK], pT[RF:P, :].bitcast(F32), ALU.subtract).then_inc(pT_done, 1)
                if on(p):
                    dve.wait_ge(log1_done, p + 1)
                    dve.wait_ge(minz_done, p + 1)
                    dve.tensor_tensor(logsig[:, :], minz[:, :, :].rearrange("p m s -> p (m s)"), log1[:, :], ALU.subtract).then_inc(logsig_done, 1)
                    dve.wait_ge(logsig_done, p + 1)
                    dve.tensor_tensor_scan(decay[:, :], carry[:, :], logsig[:, :], 0.0, ALU.mult, ALU.add).then_inc(decay_done, 1)
                if on(a):
                    dve.wait_ge(state_ps, a + 1)
                    dve.wait_ge(e01_done, a + 1)
                    for m in range(MC):
                        for j in range(2):
                            g = m * 2 + j
                            st = dve.scalar_tensor_tensor(out=state[c][:, m, j, :], in0=state[c][:, m, j, :], scalar=e01[:, g:g + 1],
                                                          in1=banks[2][:, g * dv:(g + 1) * dv], op0=ALU.mult, op1=ALU.add)
                    st.then_inc(state_done, 1)
                if on(a):
                    dve.wait_ge(rrms_done, a + 1)
                    for hh in range(2):
                        for g in range(4):
                            m, j = g // 2, g % 2
                            h = 2 * m + hh
                            yj = dve.scalar_tensor_tensor(out=y[:, j, h * dv:(h + 1) * dv], in0=banks[hh][:, g * dv:(g + 1) * dv],
                                                          scalar=rrms[:, hh * 4 + g:hh * 4 + g + 1],
                                                          in1=gate[:, j, h * dv:(h + 1) * dv], op0=ALU.mult, op1=ALU.mult)
                        yj.then_inc(y_done[hh], 1)
                if on(f):
                    for b in range(2):
                        fc = slice(2 * b, 2 * b + 2)
                        dve.wait_ge(gelu_done[b], f + 1)
                        dve.tensor_copy(hT_p[0][:, fc, :], hT[:, fc, :]).then_inc(h_hi[b], 1)
                if on(f):
                    for b in range(2, 4):
                        fc = slice(2 * b, 2 * b + 2)
                        dve.wait_ge(gelu_done[b], f + 1)
                        dve.tensor_copy(hT_p[0][:, fc, :], hT[:, fc, :]).then_inc(h_hi[b], 1)
                if on(n):
                    dve.wait_ge(rstd1_done, n + 1)
                    count_past(dve, xnT_ps, n)
                    for j in range(2):
                        xj = dve.tensor_scalar(xn[:, j, :], x_n[c][:, j, :], mv1[:, j, 0:1], rstd1[:, j:j + 1], ALU.subtract, ALU.mult)
                    xj.then_inc(xn_done, 1)
                if on(p):
                    dve.wait_ge(q_ps, p + 1)
                    dve.wait_ge(eb_done, p + 1)
                    dve.scalar_tensor_tensor(out=qg[:, :], in0=banks[4][:, :], scalar=SCALE, in1=eb[:, :], op0=ALU.mult, op1=ALU.mult).then_inc(qg_done, 1)
                    dve.wait_ge(k_ps, p + 1)
                    dve.wait_ge(enb_done, p + 1)
                    dve.tensor_tensor(kg[:, :], banks[5][:, :], enb[:, :], ALU.mult).then_inc(kg_done, 1)
                    dve.wait_ge(qg_done, p + 1)
                    dve.tensor_copy(qsc[:, :, 0, :], qgc[:, :, 0, :]).then_inc(qs0_done, 1)
                if on(a):
                    for j in range(2):
                        dve.wait_ge(yT_hi[j], a + 1)
                        dve.tensor_tensor(yT[1][:, j, :, :].rearrange("p h s -> p (h s)"), banks[6 + j][:, :],
                                          yT[0][:, j, :, :].rearrange("p h s -> p (h s)").bitcast(F32), ALU.subtract).then_inc(yT_done[j], 1)
                if on(p):
                    for j in range(2):
                        dve.wait_ge(tanh_done[j], p + 1)
                        dve.scalar_tensor_tensor(out=gate[:, j, :], in0=tanh_g[:, j, :], scalar=1.0, in1=banks[j][:, :],
                                                 op0=ALU.add, op1=ALU.mult).then_inc(gate_done[j], 1)
                if on(f):
                    dve.wait_ge(qT_ps, f + 1)
                    dve.tensor_copy(qT[0][:, :], banks[2][:, 0:TOK]).then_inc(qT_hi, 1)
                    dve.wait_ge(qT_hi, f + 1)
                    dve.tensor_tensor(qT[1][:, :], banks[2][:, 0:TOK], qT[0][:, :].bitcast(F32), ALU.subtract).then_inc(qT_done, 1)
                if on(a):
                    dve.wait_ge(proj_ps, a + 1)
                    dve.wait_ge(xres_in[c], 16 * (i + 1))
                    dve.tensor_tensor(x2[c][:, :, :].rearrange("p j d -> p (j d)"), banks[3][:, :],
                                      x_res[c][:, :, :].rearrange("p j d -> p (j d)"), ALU.add).then_inc(x2_done, 1)
                    dve.wait_ge(x2_done, a + 1)
                    for j in range(2):
                        st = dve.bn_stats(stats2[:, j, :], x2[c][:, j, :])
                    st.then_inc(stats2_done, 1)
                    dve.wait_ge(stats2_done, a + 1)
                    dve.tensor_copy(spare[:, :], stats2[:, 1, 0:1])
                    for j in range(2):
                        st = dve.bn_aggr(mv2[:, j, :], stats2[:, j, :])
                    st.then_inc(mv2_done, 1)
                if on(f):
                    dve.wait_ge(ff_ps, f + 1)
                    dve.wait_ge(x2b_done, f + 1)
                    count_past(dve, stored, 16 * f)
                    dve.tensor_tensor(res[:, :, :].rearrange("p j d -> p (j d)"), banks[4][:, :],
                                      x2b[:, :, :].rearrange("p j d -> p (j d)"), ALU.add).then_inc(res_done, 1)

            run(dve, slot, before)

        @block.tensor
        def _(pe):
            pe.wait_ge(consts, N_CONSTS)
            mm = nc.tensor.matmul

            def mm3(out, left, right, first=True, last=True):
                mm(out, left[0], right[0], start=first, stop=False)
                mm(out, left[0], right[1], start=False, stop=False)
                return mm(out, left[1], right[0], start=False, stop=last)

            def split(name, step):
                if isinstance(step, int) and step == 0:
                    pe.wait_ge(split_of[name], 1)

            def both(t, *at):
                return [x[at] for x in t]

            def slot(t, i, c):
                a, p, f = t, t + 1, t - 1
                if on(p):
                    pe.wait_ge(xn_done, p + 1)
                    count_past(pe, kg_done, p)
                    for k in range(KC):
                        for j in range(2):
                            s = nc.tensor.transpose(banks[5][:, k * TOK + j * P:k * TOK + (j + 1) * P], xn[:, j, k * P:(k + 1) * P], ident[:, :])
                    s.then_inc(xnT_ps, 1)
                if on(a):
                    pe.wait_ge(qg_done, a + 1)
                    pe.wait_ge(kg_done, a + 1)
                    pe.wait_ge(k0_done, a + 1)
                    pe.wait_ge(gate_done[0], a + 1)
                    pe.wait_ge(gate_done[1], a + 1)
                    for g in range(4):
                        m, j = g // 2, g % 2
                        for hh in range(2):
                            r, at = slice(hh * dk, hh * dk + dk), g * P
                            mm(banks[hh][:, at:at + P], kgt[r, m, j, :], qgt[r, m, j, :], start=True, stop=True)
                    for g in range(4):
                        m, j = g // 2, g % 2
                        for hh in range(2):
                            r, at = slice(hh * dk, hh * dk + dk), g * P
                            s = mm(banks[hh][0:CHUNK, at + CHUNK:at + P], k0[r, g, :], qgt[r, m, j, CHUNK:], start=True, stop=True)
                            if g == 3:
                                s.then_inc(score_ps[hh], 1)
                if on(a):
                    pe.wait_ge(kh_done, a + 1)
                    count_past(pe, qT_done, f)
                    for j in range(2):
                        for m in range(MC):
                            s = nc.tensor.transpose(banks[2][:, j * DK + m * P:j * DK + (m + 1) * P], kht_in[:, m, j, :], ident[:, :])
                    s.then_inc(kht_ps, 1)
                if on(p):
                    pe.wait_ge(xnT_done, p + 1)
                    count_past(pe, yT_done[0], a)
                    split("w1", p)
                    for k in range(KC):
                        for x in range(2):
                            s = mm(banks[6][0:4 * R, 0:TOK], w1_s[:, k, :, :, :].rearrange("p b a r -> p (b a r)"), xnT[x][:, k, :],
                                   start=(k == x == 0), stop=(k == x == 1))
                    s.then_inc(low_ps, 1)
                if on(f):
                    pe.wait_ge(x2n_done, f + 1)
                    for k in range(KC):
                        for j in range(2):
                            s = nc.tensor.transpose(banks[3][:, k * TOK + j * P:k * TOK + (j + 1) * P], x2n[:, j, k * P:(k + 1) * P], ident[:, :])
                    s.then_inc(x2nT_ps, 1)
                if on(a):
                    pe.wait_ge(v_done[0], a + 1)
                    pe.wait_ge(v_done[1], a + 1)
                    for hh in range(2):
                        pe.wait_ge(probs_done[hh], a + 1)
                        for g in range(4):
                            m, j = g // 2, g % 2
                            h = 2 * m + hh
                            mm(banks[hh][:, g * dv:(g + 1) * dv], probs[:, hh, g, :], vals[:, j, h * dv:(h + 1) * dv],
                               start=(g == 0), stop=False, skip_group_check=True)
                if on(p):
                    pe.wait_ge(low_done, p + 1)
                    if on(f):
                        pe.wait_ge(x2nT_done, f + 1)
                    split("w2", p)
                    for m in range(MC):
                        for x in range(2):
                            s = mm(banks[3][:, m * TOK:(m + 1) * TOK], w2_p[x][:, m * P:(m + 1) * P], lowT[:, :], start=(x == 0), stop=(x == 1))
                    s.then_inc(z_ps, 1)
                if on(f):
                    pe.wait_ge(x2nT_done, f + 1)
                    count_past(pe, res_done, f)
                    split("u1", f)
                    for k in range(KC):
                        s = mm3(banks[4][:, 0:TOK], both(u1_p, ALL, k), both(x2nT, ALL, k), k == 0, k == KC - 1)
                    s.then_inc(pT_ps, 1)
                if on(a):
                    pe.wait_ge(qs0_done, a + 1)
                    pe.wait_ge(qs1_done, a + 1)
                    for g in range(4):
                        m, j = g // 2, g % 2
                        for hh in range(2):
                            r = slice(hh * dk, hh * dk + dk)
                            s = mm(banks[hh][:, g * dv:(g + 1) * dv], qst[r, m, j, :], state[c][r, m, j, :],
                                   start=False, stop=True, skip_group_check=True)
                            if g == 3:
                                s.then_inc(o_ps[hh], 1)
                if on(a):
                    pe.wait_ge(kht_done, a + 1)
                    for m in range(MC):
                        for j in range(2):
                            for hh in range(2):
                                h = 2 * m + hh
                                s = mm(banks[2][hh * dk:(hh + 1) * dk, (m * 2 + j) * dv:(m * 2 + j + 1) * dv],
                                       kht[:, j, h * dk:(h + 1) * dk], vals[:, j, h * dv:(h + 1) * dv], start=True, stop=True)
                    s.then_inc(state_ps, 1)
                if on(f):
                    pe.wait_ge(pT_done, f + 1)
                    split("v1", f)
                    for b in range(4):
                        if b == 3:
                            count_past(pe, yT_done[1], a)
                        for k in range(2):
                            fc = 2 * b + k
                            for x in range(2):
                                s = mm(banks[4 + b][:, k * TOK:(k + 1) * TOK], v1_p[x][:, fc * P:(fc + 1) * P], pT[:, :], start=(x == 0), stop=(x == 1))
                        s.then_inc(h_ps[b], 1)
                if on(p):
                    split("wv", p)
                    for j in v_order(p):
                        if j == 0:
                            count_past(pe, state_done, a + 1)
                        else:
                            pe.wait_ge(minz_done, p + 1)
                        for k in range(KC):
                            s = mm3(banks[2 + j][:, :], both(xnT, ALL, k, slice(j * P, j * P + P)), both(wv_p, ALL, k), k == 0, k == KC - 1)
                        s.then_inc(v_ps[j], 1)
                    for b, w, done in ((0, wq_p, q_ps), (1, wk_p, k_ps)):
                        split("wq" if b == 0 else "wk", p)
                        if on(f):
                            pe.wait_ge(gelu_done[b], f + 1)
                        for m in range(MC):
                            for k in range(KC):
                                s = mm3(banks[4 + b][:, m * TOK:(m + 1) * TOK], both(w, ALL, k, slice(m * P, m * P + P)), both(xnT, ALL, k), k == 0, k == KC - 1)
                        s.then_inc(done, 1)
                if on(a):
                    pe.wait_ge(y_done[0], a + 1)
                    pe.wait_ge(y_done[1], a + 1)
                    for j in range(2):
                        if on(f):
                            pe.wait_ge(gelu_done[2 + j], f + 1)
                        for h in range(HEADS):
                            s = nc.tensor.transpose(banks[6 + j][:, h * P:(h + 1) * P], y[:, j, h * dv:(h + 1) * dv], ident[:, :])
                        s.then_inc(yT_ps[j], 1)
                if on(p):
                    split("wg", p)
                    for j in range(2):
                        for k in range(KC):
                            s = mm3(banks[j][:, :], both(xnT, ALL, k, slice(j * P, j * P + P)), both(wg_p, ALL, k), k == 0, k == KC - 1)
                        s.then_inc(g_ps[j], 1)
                if on(f):
                    if on(p):
                        pe.wait_ge(v_done[0], p + 1)
                    split("u2", f)
                    for b in range(4):
                        pe.wait_ge(h_lo[b], f + 1)
                        for fc in (2 * b, 2 * b + 1):
                            for x in range(2):
                                s = mm(banks[2][:, 0:TOK], u2_s[:, fc, :, :].rearrange("p a r -> p (a r)"), hT_p[x][:, fc, :],
                                       start=(fc == x == 0), stop=(fc == FC - 1 and x == 1))
                    s.then_inc(qT_ps, 1)
                if on(a):
                    if on(p):
                        pe.wait_ge(v_done[1], p + 1)
                    for j in range(2):
                        pe.wait_ge(yT_done[j], a + 1)
                        split("wo", a)
                        for h in range(HEADS):
                            s = mm3(banks[3][:, j * D:(j + 1) * D], both(yT, ALL, j, h), both(wo_p, ALL, h), h == 0, h == HEADS - 1)
                    s.then_inc(proj_ps, 1)
                if on(f):
                    if on(p):
                        pe.wait_ge(qg_done, p + 1)
                    pe.wait_ge(qT_done, f + 1)
                    split("v2", f)
                    for j in range(2):
                        s = mm3(banks[4][:, j * D:(j + 1) * D], both(qT, ALL, slice(j * P, j * P + P)), both(v2_p, ALL, ALL))
                    s.then_inc(ff_ps, 1)

            run(pe, slot)


_INS = ['L0_attn_x', 'L0_attn_Wq', 'L0_attn_Wk', 'L0_attn_Wv', 'L0_attn_Wg', 'L0_attn_gk_w1', 'L0_attn_gk_w2', 'L0_attn_gk_b2',
        'L0_attn_g_norm_w', 'L0_attn_Wo', 'L0_ffn_U1', 'L0_ffn_V1', 'L0_ffn_b1', 'L0_ffn_U2', 'L0_ffn_V2', 'L0_ffn_b2']

_COLUMNS = ['L0_attn_gk_b2', 'L0_ffn_b1']


def kernel(**inputs):
    import numpy as _np
    import concourse.bacc as _bacc
    from concourse import mybir as _mybir
    from concourse.bass_utils import run_bass_kernel_spmd as _run

    nc = _bacc.Bacc("TRN2", target_bir_lowering=False, num_devices=1)
    arrays, args = {}, []
    for name in _INS:
        a = _np.asarray(inputs[name])
        if name in _COLUMNS:
            a = a.reshape(-1, P).T
        a = _np.ascontiguousarray(a)
        arrays[f"in_{name}_dram"] = a
        args.append(nc.dram_tensor(f"in_{name}_dram", a.shape, _mybir.dt.from_np(a.dtype), kind="ExternalInput").ap())
    args.append(nc.dram_tensor("out_dram", inputs['L0_attn_x'].shape, _mybir.dt.float32, kind="ExternalOutput").ap())
    build(nc, *args)
    r = _run(nc, [arrays], core_ids=[0])
    return r.results[0]["out_dram"]
```

```python
from contextlib import ExitStack

from concourse import mybir

ALU = mybir.AluOpType
ACT = mybir.ActivationFunctionType
F32 = mybir.dt.float32
F32R = mybir.dt.float32r

P = 128
ALL = slice(None)
CHUNK = 64
HEADS = 4
GATE_NORM = 16.0
EPS = 1e-5


def count_past(eng, sem, n):
    if not isinstance(n, int) or n > 0:
        eng.wait_ge(sem, n)


def build(nc, x, Wq, Wk, Wv, Wg, gk_w1, gk_w2, gk_b2, g_norm_w, Wo, U1, V1, b1, U2, V2, b2, out):
    B, L, D = x.shape
    DK = Wq.shape[1]
    DV = Wv.shape[1]
    R = gk_w1.shape[1]
    dk, dv = DK // HEADS, DV // HEADS
    RF, FF = V1.shape
    KC = D // P
    MC = DK // P
    FC = FF // P
    PAIRS = B // 2
    STEPS = PAIRS * L // P
    TOK = 2 * P
    SCALE = float(dk) ** -0.5
    assert (KC, MC, dv, dk, FC, PAIRS) == (2, 2, 128, 64, 8, 2)

    with ExitStack() as ctx:
        def sb(name, *shape):
            return ctx.enter_context(nc.sbuf_tensor(name, list(shape), F32))

        def sem(name):
            return ctx.enter_context(nc.semaphore(name))

        banks = [ctx.enter_context(nc.psum_tensor(f"bank{i}", [P, 512], F32)) for i in range(8)]

        def parts(name, *shape):
            return [ctx.enter_context(nc.sbuf_tensor(f"{name}_{x}", list(shape), F32R)) for x in ("hi", "lo")]

        wq, wk = sb("wq", P, KC, DK), sb("wk", P, KC, DK)
        wv, wg = sb("wv", P, KC, DV), sb("wg", P, KC, DV)
        w1, w2 = sb("w1", P, KC, R), sb("w2", P, DK)
        wo = sb("wo", P, HEADS, D)
        u1, v1 = sb("u1", P, KC, RF), sb("v1", P, FF)
        u2, v2 = sb("u2", P, FC, RF), sb("v2", P, D)
        wq_p, wk_p = parts("wq", P, KC, DK), parts("wk", P, KC, DK)
        wv_p, wg_p = parts("wv", P, KC, DV), parts("wg", P, KC, DV)
        wo_p, v1_p, u1_p = parts("wo", P, HEADS, D), parts("v1", P, FF), parts("u1", P, KC, 2, RF)
        v2_p = parts("v2", P, D)
        w2_s = ctx.enter_context(nc.sbuf_tensor("w2_s", [P, DK], F32R))
        w1_s = ctx.enter_context(nc.sbuf_tensor("w1_s", [P, KC, 4, 2, R], F32R))
        u2_s = ctx.enter_context(nc.sbuf_tensor("u2_s", [P, FC, 2, RF], F32R))
        gate_bias = sb("gate_bias", P, MC)
        norm_w = sb("norm_w", P, 1)
        ff_bias = sb("ff_bias", P, FC)
        out_bias = sb("out_bias", P, D)
        ident = sb("ident", P, P)
        causal = sb("causal", P, P)
        carry = sb("carry", P, MC * TOK)
        neg_half, eps, eps_sum = sb("neg_half", P, HEADS), sb("eps", P, 2), sb("eps_sum", P, HEADS)

        x_n = [sb(f"x_n{c}", P, 2, D) for c in range(2)]
        x_res = [sb(f"x_res{c}", P, 2, D) for c in range(2)]
        stats1, mv1, rstd1 = sb("stats1", P, 2, 6), sb("mv1", P, 2, 2), sb("rstd1", P, 2)
        var1 = sb("var1", P, 2)
        spare = sb("spare", P, 1)
        xn = sb("xn", P, 2, D)
        xnT = parts("xnT", P, KC, TOK)
        lowT = ctx.enter_context(nc.sbuf_tensor("lowT", [P, TOK], F32R))
        absz, expz, log1 = sb("absz", P, MC, TOK), sb("expz", P, MC * TOK), sb("log1", P, MC * TOK)
        minz = sb("minz", P, MC, TOK)
        logsig, decay = sb("logsig", P, MC * TOK), sb("decay", P, MC * TOK)
        eb, enb = sb("eb", P, MC * TOK), sb("enb", P, MC * TOK)
        qg, kg = sb("qg", P, MC * TOK), sb("kg", P, MC * TOK)
        qs, kh = sb("qs", P, MC * TOK), sb("kh", P, MC * TOK)
        k0 = sb("k0", P, MC * 2, CHUNK)
        e01 = sb("e01", P, MC * 2)
        kht = sb("kht", P, 2, DK)
        vals = sb("vals", P, 2, DV)
        tanh_g, gate = sb("tanh_g", P, 2, DV), sb("gate", P, 2, DV)
        probs = sb("probs", P, 2, HEADS, P)
        state = [sb(f"state{c}", P, MC, 2, dv) for c in range(2)]
        sq, ssq = sb("sq", P, 2, HEADS * dv), sb("ssq", P, 2 * HEADS)
        meansq, rrms = sb("meansq", P, 2 * HEADS), sb("rrms", P, 2 * HEADS)
        y = sb("y", P, 2, DV)
        yT = parts("yT", P, 2, HEADS, P)
        x2 = [sb(f"x2_{c}", P, 2, D) for c in range(2)]
        x2b = sb("x2b", P, 2, D)
        stats2, mv2, rstd2 = sb("stats2", P, 2, 6), sb("mv2", P, 2, 2), sb("rstd2", P, 2)
        var2 = sb("var2", P, 2)
        x2n = sb("x2n", P, 2, D)
        x2nT = parts("x2nT", P, KC, TOK)
        pT = ctx.enter_context(nc.sbuf_tensor("pT", [P, TOK], F32R))
        hT, hT_p = sb("hT", P, FC, TOK), parts("hT", P, FC, TOK)
        qT = parts("qT", P, TOK)
        res = sb("res", P, 2, D)

        def by_chunk(t):
            return t[:, :].rearrange("p (g c s) -> p g c s", c=2, s=CHUNK)

        def by_tile(t):
            return t[:, :].rearrange("p (m j s) -> p m j s", m=MC, j=2)

        ebc, kgc, qgc, qsc, khc = (by_chunk(t) for t in (eb, kg, qg, qs, kh))
        qgt, kgt, qst, kht_in = (by_tile(t) for t in (qg, kg, qs, kh))
        last = CHUNK - 1

        def over_chunk(col):
            return col.to_broadcast([P, MC * 2, CHUNK])

        consts = sem("consts")
        wo_scaled = sem("wo_scaled")
        names = ("w1", "w2", "zb", "wv", "wq", "wk", "wg", "nw", "wo", "u1", "v1", "u2", "v2", "fb", "b2")
        in_of = {n: sem(f"in_{n}") for n in names}
        hi_of = {n: sem(f"hi_{n}") for n in ("w1", "w2", "wv", "wq", "wk", "wg", "wo", "u1", "v1", "u2", "v2")}
        split_of = {n: sem(f"split_{n}") for n in hi_of}
        x_in = [sem(f"x_in{c}") for c in range(2)]
        xres_in = [sem(f"xres_in{c}") for c in range(2)]
        stats1_done, mv1_done, var1_done, rstd1_done, xn_done = map(
            sem, ("stats1_done", "mv1_done", "var1_done", "rstd1_done", "xn_done"))
        xnT_ps, xnT_hi, xnT_done = sem("xnT_ps"), sem("xnT_hi"), sem("xnT_done")
        low_ps, low_hi, low_done = sem("low_ps"), sem("low_hi"), sem("low_done")
        z_ps, absz_done, expz_done, log1_done = map(sem, ("z_ps", "absz_done", "expz_done", "log1_done"))
        minz_done, logsig_done, decay_done = map(sem, ("minz_done", "logsig_done", "decay_done"))
        eb_done, enb_done = sem("eb_done"), sem("enb_done")
        v_ps, v_done = [sem(f"v_ps{j}") for j in range(2)], [sem(f"v_done{j}") for j in range(2)]
        q_ps, k_ps, qg_done, kg_done = map(sem, ("q_ps", "k_ps", "qg_done", "kg_done"))
        k0_done, kh_done, qs0_done, qs1_done, e01_done = map(
            sem, ("k0_done", "kh_done", "qs0_done", "qs1_done", "e01_done"))
        g_ps, tanh_done, gate_done = ([sem(f"{n}{j}") for j in range(2)] for n in ("g_ps", "tanh_done", "gate_done"))
        score_ps, probs_done = ([sem(f"{n}{j}") for j in range(2)] for n in ("score_ps", "probs_done"))
        kht_ps, kht_done = sem("kht_ps"), sem("kht_done")
        o_ps, ssq_done, y_done = ([sem(f"{n}{j}") for j in range(2)] for n in ("o_ps", "ssq_done", "y_done"))
        state_ps, state_done = sem("state_ps"), sem("state_done")
        meansq_done, rrms_done = ([sem(f"{n}{hh}") for hh in range(2)] for n in ("meansq_done", "rrms_done"))
        yT_ps, yT_hi, yT_done = ([sem(f"{n}{j}") for j in range(2)] for n in ("yT_ps", "yT_hi", "yT_done"))
        proj_ps, x2_done = ([sem(f"{n}{j}") for j in range(2)] for n in ("proj_ps", "x2_done"))
        x2b_done = sem("x2b_done")
        stats2_done, mv2_done, var2_done, rstd2_done, x2n_done = map(
            sem, ("stats2_done", "mv2_done", "var2_done", "rstd2_done", "x2n_done"))
        x2nT_ps, x2nT_hi, x2nT_done, pT_ps, pT_hi, pT_done = map(
            sem, ("x2nT_ps", "x2nT_hi", "x2nT_done", "pT_ps", "pT_hi", "pT_done"))
        h_ps, gelu_done, h_hi, h_lo = ([sem(f"{n}{b}") for b in range(4)] for n in ("h_ps", "gelu_done", "h_hi", "h_lo"))
        qT_ps, qT_hi, qT_done, ff_ps, res_done, stored = map(sem, ("qT_ps", "qT_hi", "qT_done", "ff_ps", "res_done", "stored"))

        x_dram = x.rearrange("(c j) (i p) d -> c i p j d", c=PAIRS, p=P)
        out_dram = out.rearrange("(c j) (i p) d -> c i p j d", c=PAIRS, p=P)

        def rows(w, n):
            return w.rearrange("(k p) n -> p k n", k=n)

        loads = [
            ("w1", w1[:, :, :], rows(gk_w1, KC)),
            ("w2", w2[:, :], gk_w2.rearrange("(a r) d -> a r d", a=1).to_broadcast([P // R, R, DK])),
            ("zb", gate_bias[:, :], gk_b2),
            ("wv", wv[:, :, :], rows(Wv, KC)), ("wq", wq[:, :, :], rows(Wq, KC)), ("wk", wk[:, :, :], rows(Wk, KC)),
            ("wg", wg[:, :, :], rows(Wg, KC)),
            ("nw", norm_w[:, :], g_norm_w.rearrange("(p a) -> p a", a=1)),
            ("wo", wo[:, :, :], rows(Wo, HEADS)),
            ("u1", u1[:, :, :], rows(U1, KC)),
            ("v1", v1[0:RF, :], V1), ("v1", v1[RF:P, :], V1),
            ("u2", u2[:, :, :], rows(U2, FC)),
            ("v2", v2[0:RF, :], V2), ("v2", v2[RF:P, :], V2),
            ("fb", ff_bias[:, :], b1),
            ("b2", out_bias[:, :], b2.rearrange("(a d) -> a d", a=1).to_broadcast([P, D])),
        ]

        def arrived(eng, name):
            eng.wait_ge(in_of[name], 16 * sum(n == name for n, _, _ in loads))

        flat = {
            "w1": (w1[:, :, :].unsqueeze(2).to_broadcast([P, KC, 4, R]), w1_s[:, :, :, 0, :], w1_s[:, :, :, 1, :]),
            "w2": (w2[:, :], w2_s[:, :], None),
            "wv": (wv[:, :, :], wv_p[0][:, :, :], wv_p[1][:, :, :]),
            "wq": (wq[:, :, :], wq_p[0][:, :, :], wq_p[1][:, :, :]),
            "wk": (wk[:, :, :], wk_p[0][:, :, :], wk_p[1][:, :, :]),
            "wg": (wg[:, :, :], wg_p[0][:, :, :], wg_p[1][:, :, :]),
            "wo": (wo[:, :, :], wo_p[0][:, :, :], wo_p[1][:, :, :]),
            "u1": (u1[:, :, :].unsqueeze(2).to_broadcast([P, KC, 2, RF]), u1_p[0][:, :, :, :], u1_p[1][:, :, :, :]),
            "v1": (v1[:, :], v1_p[0][:, :], v1_p[1][:, :]),
            "u2": (u2[:, :, :], u2_s[:, :, 0, :], u2_s[:, :, 1, :]),
            "v2": (v2[:, :], v2_p[0][:, :], v2_p[1][:, :]),
        }

        def weight_hi(act, name):
            arrived(act, name)
            if name == "wo":
                act.wait_ge(wo_scaled, 1)
            act.activation(flat[name][1], flat[name][0], ACT.Copy).then_inc(hi_of[name], 1)

        def weight_lo(eng, name):
            eng.wait_ge(hi_of[name], 1)
            if name == "w2":
                for r in (slice(2 * R, 4 * R), slice(6 * R, 8 * R)):
                    lo = eng.tensor_tensor(w2_s[r, :], w2[r, :], w2_s[r, :].bitcast(F32), ALU.subtract)
                lo.then_inc(split_of[name], 1)
                return
            eng.tensor_tensor(flat[name][2], flat[name][0], flat[name][1].bitcast(F32), ALU.subtract).then_inc(split_of[name], 1)

        def h_lo_part(eng, f, b):
            eng.wait_ge(h_hi[b], f + 1)
            fc = slice(2 * b, 2 * b + 2)
            eng.tensor_tensor(hT_p[1][:, fc, :], hT[:, fc, :], hT_p[0][:, fc, :].bitcast(F32), ALU.subtract).then_inc(h_lo[b], 1)

        N_CONSTS = 11

        def on(step):
            return not isinstance(step, int) or 0 <= step < STEPS

        def first(step):
            return isinstance(step, int) and step == 0

        def has_past(step):
            return not isinstance(step, int) or step >= PAIRS

        def has_future(step):
            return not isinstance(step, int) or step < STEPS - PAIRS

        def dve_takes_lo(step, b):
            return isinstance(step, int) and step >= STEPS - 2 and b % 2 == 1

        def v_order(step):
            return (0, 1) if first(step) else (1, 0)

        def run(eng, slot, before=None):
            for t in range(-2, 2):
                if before is not None:
                    before(t)
                slot(t, t // 2, t % 2)
            with eng.Fori(1, STEPS // 2 - 1) as i:
                for c in range(2):
                    slot(2 * i + c, i, c)
            for t in range(STEPS - 2, STEPS + 1):
                slot(t, t // 2, t % 2)

        block = ctx.enter_context(nc.Block())

        @block.sync
        def _(sp):
            def before(t):
                for name, dst, src in {-1: loads[:5], 0: loads[5:]}.get(t, ()):
                    sp.dma_start(dst, src).then_inc(in_of[name], 16)

            def load_x(s, i, c):
                count_past(sp, xn_done, s - 1)
                sp.dma_start(x_n[c][:, :, :], x_dram[c, i]).then_inc(x_in[c], 16)

            def slot(t, i, c):
                if on(t + 2):
                    load_x(t + 2, i + 1, c)
                if on(t):
                    count_past(sp, x2_done[1], t - 1)
                    sp.dma_start(x_res[c][:, :, :], x_dram[c, i]).then_inc(xres_in[c], 16)
                if on(t - 1):
                    j = i - 1 + c
                    sp.wait_ge(res_done, t)
                    sp.dma_start(out_dram[1 - c, j], res[:, :, :]).then_inc(stored, 16)

            run(sp, slot, before)
            sp.wait_ge(stored, 16 * STEPS)

        @block.gpsimd
        def _(pool):
            pool.memset(neg_half[:, :], -0.5).then_inc(consts, 1)
            pool.memset(eps[:, :], EPS).then_inc(consts, 1)
            pool.memset(eps_sum[:, :], EPS * dv).then_inc(consts, 1)
            pool.memset(ident[:, :], 0.0).then_inc(consts, 1)
            pool.memset(causal[:, :], 1.0).then_inc(consts, 1)
            pool.wait_ge(consts, 8)
            pool.affine_select(out=ident[:, :], in_=ident[:, :], compare_op=ALU.not_equal, fill=1.0,
                               base=0, pattern=[[-1, P]], channel_multiplier=1).then_inc(consts, 1)
            pool.affine_select(out=causal[:, :], in_=causal[:, :], compare_op=ALU.is_ge, fill=0.0,
                               base=0, pattern=[[1, P]], channel_multiplier=-1).then_inc(consts, 1)

            def before(t):
                for name in {-1: ("w1", "wv"), 0: ("wo",), 1: ("u1", "v1", "u2", "v2")}.get(t, ()):
                    weight_lo(pool, name)

            def slot(t, i, c):
                a, p, f, n = t, t + 1, t - 1, t + 2
                if on(n):
                    pool.wait_ge(mv1_done, n + 1)
                    pool.tensor_tensor(var1[:, :], mv1[:, :, 1], eps[:, 0:2], ALU.add).then_inc(var1_done, 1)
                    pool.wait_ge(var1_done, n + 1)
                    pool.tensor_tensor(rstd1[:, :], var1[:, :], neg_half[:, 0:2], ALU.pow).then_inc(rstd1_done, 1)
                if on(a):
                    for hh in range(2):
                        mine = slice(hh * HEADS, (hh + 1) * HEADS)
                        pool.wait_ge(ssq_done[hh], a + 1)
                        pool.tensor_tensor(meansq[:, mine], ssq[:, mine], eps_sum[:, :], ALU.add).then_inc(meansq_done[hh], 1)
                        pool.wait_ge(meansq_done[hh], a + 1)
                        pool.tensor_tensor(rrms[:, mine], meansq[:, mine], neg_half[:, :], ALU.pow).then_inc(rrms_done[hh], 1)
                if on(f):
                    for b in range(4):
                        if not dve_takes_lo(f, b):
                            h_lo_part(pool, f, b)
                if on(p):
                    if first(p):
                        weight_lo(pool, "wk")
                        weight_lo(pool, "wg")
                    if has_future(p):
                        pool.wait_ge(eb_done, p + 1)
                        count_past(pool, state_done, p)
                        pool.tensor_tensor(e01[:, :], ebc[:, :, 0, last], ebc[:, :, 1, last], ALU.mult).then_inc(e01_done, 1)
                    pool.wait_ge(qg_done, p + 1)
                    pool.tensor_tensor(qsc[:, :, 1, :], qgc[:, :, 1, :], over_chunk(ebc[:, :, 0, last:]), ALU.mult).then_inc(qs1_done, 1)
                    pool.wait_ge(kg_done, p + 1)
                    pool.tensor_tensor(k0[:, :, :], kgc[:, :, 0, :], over_chunk(ebc[:, :, 0, last:]), ALU.mult).then_inc(k0_done, 1)
                    if has_future(p):
                        pool.tensor_tensor(khc[:, :, 1, :], kgc[:, :, 1, :], over_chunk(ebc[:, :, 1, last:]), ALU.mult)
                        pool.wait_ge(k0_done, p + 1)
                        pool.tensor_tensor(khc[:, :, 0, :], k0[:, :, :], over_chunk(ebc[:, :, 1, last:]), ALU.mult).then_inc(kh_done, 1)
                if on(a):
                    pool.wait_ge(mv2_done, a + 1)
                    pool.tensor_tensor(var2[:, :], mv2[:, :, 1], eps[:, 0:2], ALU.add).then_inc(var2_done, 1)
                    pool.wait_ge(var2_done, a + 1)
                    pool.tensor_tensor(rstd2[:, :], var2[:, :], neg_half[:, 0:2], ALU.pow).then_inc(rstd2_done, 1)
                    count_past(pool, res_done, a)
                    if first(a):
                        arrived(pool, "b2")
                    pool.tensor_tensor(x2b[:, :, :], x2[c][:, :, :], out_bias[:, :].unsqueeze(1).to_broadcast([P, 2, D]), ALU.add).then_inc(x2b_done, 1)

            run(pool, slot, before)

        @block.scalar
        def _(act):
            def before(t):
                for name in {-1: ("w1", "w2"), 1: ("u2", "v2")}.get(t, ()):
                    weight_hi(act, name)

            def slot(t, i, c):
                a, p, f = t, t + 1, t - 1
                if on(p):
                    act.wait_ge(xnT_ps, p + 1)
                    act.activation(xnT[0][:, :, :].rearrange("p k s -> p (k s)"), banks[5][:, :], ACT.Copy).then_inc(xnT_hi, 1)
                    if first(p):
                        for name in ("wv", "wq", "wk"):
                            weight_hi(act, name)
                if on(a) and has_future(a):
                    act.wait_ge(kht_ps, a + 1)
                    act.activation(kht[:, :, :].rearrange("p j d -> p (j d)"), banks[2][:, :], ACT.Copy).then_inc(kht_done, 1)
                if on(f):
                    act.wait_ge(x2nT_ps, f + 1)
                    act.activation(x2nT[0][:, :, :].rearrange("p k s -> p (k s)"), banks[3][:, :], ACT.Copy).then_inc(x2nT_hi, 1)
                if on(p):
                    if first(p):
                        arrived(act, "zb")
                    act.preload_act_table_set("natural_log_exp_and_others")
                    act.wait_ge(z_ps, p + 1)
                    for m in range(MC):
                        zabs = act.activation(absz[:, m, :], banks[3][:, m * TOK:(m + 1) * TOK], ACT.Abs, bias=gate_bias[:, m:m + 1])
                    zabs.then_inc(absz_done, 1)
                    act.wait_ge(absz_done, p + 1)
                    act.activation(expz[:, :], absz[:, :, :].rearrange("p m s -> p (m s)"), ACT.Exp, scale=-1.0).then_inc(expz_done, 1)
                    act.wait_ge(expz_done, p + 1)
                    act.activation(log1[:, :], expz[:, :], ACT.Ln, bias=1.0).then_inc(log1_done, 1)
                    if first(p):
                        weight_hi(act, "wg")
                if on(a):
                    for hh in range(2):
                        act.wait_ge(o_ps[hh], a + 1)
                        for g in range(4):
                            e = slice(g * dv, (g + 1) * dv)
                            sq_sum = act.activation(sq[:, hh, e], banks[hh][:, e], ACT.Square, accum_out=ssq[:, hh * 4 + g:hh * 4 + g + 1])
                        sq_sum.then_inc(ssq_done[hh], 1)
                if on(p):
                    act.wait_ge(decay_done, p + 1)
                    act.activation(eb[:, :], decay[:, :], ACT.Exp, scale=1.0 / GATE_NORM).then_inc(eb_done, 1)
                    act.activation(enb[:, :], decay[:, :], ACT.Exp, scale=-1.0 / GATE_NORM).then_inc(enb_done, 1)
                if on(f):
                    if first(f):
                        arrived(act, "fb")
                    for b in range(4):
                        act.wait_ge(h_ps[b], f + 1)
                        for k in range(2):
                            fc = 2 * b + k
                            g = act.activation(hT[:, fc, :], banks[4 + b][:, k * TOK:(k + 1) * TOK], ACT.Gelu_apprx_tanh, bias=ff_bias[:, fc:fc + 1])
                        g.then_inc(gelu_done[b], 1)
                if on(p):
                    for j in v_order(p):
                        act.wait_ge(v_ps[j], p + 1)
                        act.activation(vals[:, j, :], banks[2 + j][:, :], ACT.Copy).then_inc(v_done[j], 1)
                    if first(p):
                        for name in ("wo", "u1", "v1"):
                            weight_hi(act, name)
                if on(a):
                    for j in range(2):
                        act.wait_ge(yT_ps[j], a + 1)
                        act.activation(yT[0][:, j, :, :].rearrange("p h s -> p (h s)"), banks[6 + j][:, :], ACT.Copy).then_inc(yT_hi[j], 1)
                if on(p):
                    for j in range(2):
                        act.wait_ge(g_ps[j], p + 1)
                        act.activation(tanh_g[:, j, :], banks[j][:, :], ACT.Tanh, scale=0.5).then_inc(tanh_done[j], 1)

            run(act, slot, before)

        @block.vector
        def _(dve):
            dve.memset(carry[:, :], 1.0).then_inc(consts, 1)
            dve.memset(state[0][:, :, :, :], 0.0).then_inc(consts, 1)
            dve.memset(state[1][:, :, :, :], 0.0).then_inc(consts, 1)
            dve.wait_ge(consts, 8)
            dve.memset(carry[:, :].rearrange("p (g s) -> p g s", s=CHUNK)[:, :, 0:1], 0.0).then_inc(consts, 1)
            dve.wait_ge(consts, N_CONSTS)

            def slot(t, i, c):
                a, p, f, n = t, t + 1, t - 1, t + 2
                if on(p):
                    dve.wait_ge(xnT_hi, p + 1)
                    dve.tensor_tensor(xnT[1][:, :, :].rearrange("p k s -> p (k s)"), banks[5][:, :],
                                      xnT[0][:, :, :].rearrange("p k s -> p (k s)").bitcast(F32), ALU.subtract).then_inc(xnT_done, 1)
                if on(f):
                    dve.wait_ge(rstd2_done, f + 1)
                    for j in range(2):
                        xj = dve.tensor_scalar(x2n[:, j, :], x2[1 - c][:, j, :], mv2[:, j, 0:1], rstd2[:, j:j + 1], ALU.subtract, ALU.mult)
                    xj.then_inc(x2n_done, 1)
                if on(a):
                    for hh in range(2):
                        dve.wait_ge(score_ps[hh], a + 1)
                        dve.tensor_tensor(probs[:, hh, :, :], banks[hh][:, :].rearrange("p (g s) -> p g s", g=4),
                                          causal[:, :].unsqueeze(1).to_broadcast([P, 4, P]), ALU.mult).then_inc(probs_done[hh], 1)
                if on(p):
                    if first(p):
                        weight_lo(dve, "w2")
                    dve.wait_ge(low_ps, p + 1)
                    dve.tensor_copy(lowT[:, :], banks[6][:, 0:TOK]).then_inc(low_hi, 1)
                    dve.wait_ge(low_hi, p + 1)
                    dve.tensor_tensor(lowT[P // 2:P, :], banks[6][P // 2:P, 0:TOK], lowT[P // 2:P, :].bitcast(F32), ALU.subtract).then_inc(low_done, 1)
                if on(f):
                    dve.wait_ge(x2nT_hi, f + 1)
                    dve.tensor_tensor(x2nT[1][:, :, :].rearrange("p k s -> p (k s)"), banks[3][:, :],
                                      x2nT[0][:, :, :].rearrange("p k s -> p (k s)").bitcast(F32), ALU.subtract).then_inc(x2nT_done, 1)
                if on(n):
                    dve.wait_ge(x_in[c], 16 * (i + 2))
                    for j in range(2):
                        st = dve.bn_stats(stats1[:, j, :], x_n[c][:, j, :])
                    st.then_inc(stats1_done, 1)
                    dve.wait_ge(stats1_done, n + 1)
                    dve.tensor_copy(spare[:, :], stats1[:, 1, 0:1])
                    for j in range(2):
                        st = dve.bn_aggr(mv1[:, j, :], stats1[:, j, :])
                    st.then_inc(mv1_done, 1)
                if on(p):
                    if first(p):
                        weight_lo(dve, "wq")
                    dve.wait_ge(absz_done, p + 1)
                    for m in range(MC):
                        mz = dve.tensor_scalar(minz[:, m, :], banks[3][:, m * TOK:(m + 1) * TOK], gate_bias[:, m:m + 1], 0.0, ALU.add, ALU.min)
                    mz.then_inc(minz_done, 1)
                if on(f):
                    dve.wait_ge(pT_ps, f + 1)
                    dve.tensor_copy(pT[:, :], banks[4][:, 0:TOK]).then_inc(pT_hi, 1)
                    dve.wait_ge(pT_hi, f + 1)
                    dve.tensor_tensor(pT[RF:P, :], banks[4][RF:P, 0:TOK], pT[RF:P, :].bitcast(F32), ALU.subtract).then_inc(pT_done, 1)
                if on(p):
                    dve.wait_ge(log1_done, p + 1)
                    dve.wait_ge(minz_done, p + 1)
                    dve.tensor_tensor(logsig[:, :], minz[:, :, :].rearrange("p m s -> p (m s)"), log1[:, :], ALU.subtract).then_inc(logsig_done, 1)
                    dve.wait_ge(logsig_done, p + 1)
                    dve.tensor_tensor_scan(decay[:, :], carry[:, :], logsig[:, :], 0.0, ALU.mult, ALU.add).then_inc(decay_done, 1)
                if on(a) and has_future(a):
                    dve.wait_ge(state_ps, a + 1)
                    dve.wait_ge(e01_done, a + 1)
                    for m in range(MC):
                        for j in range(2):
                            g = m * 2 + j
                            st = dve.scalar_tensor_tensor(out=state[c][:, m, j, :], in0=state[c][:, m, j, :], scalar=e01[:, g:g + 1],
                                                          in1=banks[2][:, g * dv:(g + 1) * dv], op0=ALU.mult, op1=ALU.add)
                    st.then_inc(state_done, 1)
                if on(a):
                    for hh in range(2):
                        dve.wait_ge(rrms_done[hh], a + 1)
                        for g in range(4):
                            m, j = g // 2, g % 2
                            h = 2 * m + hh
                            yj = dve.scalar_tensor_tensor(out=y[:, j, h * dv:(h + 1) * dv], in0=banks[hh][:, g * dv:(g + 1) * dv],
                                                          scalar=rrms[:, hh * 4 + g:hh * 4 + g + 1],
                                                          in1=gate[:, j, h * dv:(h + 1) * dv], op0=ALU.mult, op1=ALU.mult)
                        yj.then_inc(y_done[hh], 1)
                if on(f):
                    for b in range(4):
                        fc = slice(2 * b, 2 * b + 2)
                        dve.wait_ge(gelu_done[b], f + 1)
                        dve.tensor_copy(hT_p[0][:, fc, :], hT[:, fc, :]).then_inc(h_hi[b], 1)
                        if dve_takes_lo(f, b):
                            h_lo_part(dve, f, b)
                if on(n):
                    dve.wait_ge(rstd1_done, n + 1)
                    count_past(dve, xnT_ps, n)
                    for j in range(2):
                        xj = dve.tensor_scalar(xn[:, j, :], x_n[c][:, j, :], mv1[:, j, 0:1], rstd1[:, j:j + 1], ALU.subtract, ALU.mult)
                    xj.then_inc(xn_done, 1)
                if on(p):
                    if first(p):
                        arrived(dve, "nw")
                        arrived(dve, "wo")
                        dve.tensor_scalar(wo[:, :, :], wo[:, :, :], norm_w[:, 0:1], 0.5 * float(dv) ** 0.5, ALU.mult, ALU.mult).then_inc(wo_scaled, 1)
                    dve.wait_ge(q_ps, p + 1)
                    dve.wait_ge(eb_done, p + 1)
                    dve.scalar_tensor_tensor(out=qg[:, :], in0=banks[4][:, :], scalar=SCALE, in1=eb[:, :], op0=ALU.mult, op1=ALU.mult).then_inc(qg_done, 1)
                    dve.wait_ge(k_ps, p + 1)
                    dve.wait_ge(enb_done, p + 1)
                    dve.tensor_tensor(kg[:, :], banks[5][:, :], enb[:, :], ALU.mult).then_inc(kg_done, 1)
                    dve.wait_ge(qg_done, p + 1)
                    dve.tensor_copy(qsc[:, :, 0, :], qgc[:, :, 0, :]).then_inc(qs0_done, 1)
                if on(a):
                    for j in range(2):
                        dve.wait_ge(yT_hi[j], a + 1)
                        dve.tensor_tensor(yT[1][:, j, :, :].rearrange("p h s -> p (h s)"), banks[6 + j][:, :],
                                          yT[0][:, j, :, :].rearrange("p h s -> p (h s)").bitcast(F32), ALU.subtract).then_inc(yT_done[j], 1)
                if on(p):
                    for j in range(2):
                        dve.wait_ge(tanh_done[j], p + 1)
                        dve.scalar_tensor_tensor(out=gate[:, j, :], in0=tanh_g[:, j, :], scalar=1.0, in1=banks[j][:, :],
                                                 op0=ALU.add, op1=ALU.mult).then_inc(gate_done[j], 1)
                if on(f):
                    dve.wait_ge(qT_ps, f + 1)
                    dve.tensor_copy(qT[0][:, :], banks[2][:, 0:TOK]).then_inc(qT_hi, 1)
                    dve.wait_ge(qT_hi, f + 1)
                    dve.tensor_tensor(qT[1][:, :], banks[2][:, 0:TOK], qT[0][:, :].bitcast(F32), ALU.subtract).then_inc(qT_done, 1)
                if on(a):
                    dve.wait_ge(xres_in[c], 16 * (i + 1))
                    for j in range(2):
                        dve.wait_ge(proj_ps[j], a + 1)
                        dve.tensor_tensor(x2[c][:, j, :], banks[3 + 3 * j][:, 0:D], x_res[c][:, j, :], ALU.add).then_inc(x2_done[j], 1)
                        dve.wait_ge(x2_done[j], a + 1)
                        st = dve.bn_stats(stats2[:, j, :], x2[c][:, j, :])
                    st.then_inc(stats2_done, 1)
                    dve.wait_ge(stats2_done, a + 1)
                    dve.tensor_copy(spare[:, :], stats2[:, 1, 0:1])
                    for j in range(2):
                        st = dve.bn_aggr(mv2[:, j, :], stats2[:, j, :])
                    st.then_inc(mv2_done, 1)
                if on(f):
                    dve.wait_ge(ff_ps, f + 1)
                    dve.wait_ge(x2b_done, f + 1)
                    count_past(dve, stored, 16 * f)
                    dve.tensor_tensor(res[:, :, :].rearrange("p j d -> p (j d)"), banks[4][:, :],
                                      x2b[:, :, :].rearrange("p j d -> p (j d)"), ALU.add).then_inc(res_done, 1)

            run(dve, slot)

        @block.tensor
        def _(pe):
            pe.wait_ge(consts, N_CONSTS)
            mm = nc.tensor.matmul

            def mm3(out, left, right, first=True, last=True):
                mm(out, left[0], right[0], start=first, stop=False)
                mm(out, left[0], right[1], start=False, stop=False)
                return mm(out, left[1], right[0], start=False, stop=last)

            def split(name, step):
                if first(step):
                    pe.wait_ge(split_of[name], 1)

            def both(t, *at):
                return [x[at] for x in t]

            def slot(t, i, c):
                a, p, f = t, t + 1, t - 1
                if on(p):
                    pe.wait_ge(xn_done, p + 1)
                    count_past(pe, kg_done, p)
                    for k in range(KC):
                        for j in range(2):
                            s = nc.tensor.transpose(banks[5][:, k * TOK + j * P:k * TOK + (j + 1) * P], xn[:, j, k * P:(k + 1) * P], ident[:, :])
                    s.then_inc(xnT_ps, 1)
                if on(a):
                    pe.wait_ge(qg_done, a + 1)
                    pe.wait_ge(kg_done, a + 1)
                    pe.wait_ge(k0_done, a + 1)
                    pe.wait_ge(gate_done[0], a + 1)
                    pe.wait_ge(gate_done[1], a + 1)
                    for g in range(4):
                        m, j = g // 2, g % 2
                        for hh in range(2):
                            r, at = slice(hh * dk, hh * dk + dk), g * P
                            mm(banks[hh][:, at:at + P], kgt[r, m, j, :], qgt[r, m, j, :], start=True, stop=True)
                    for g in range(4):
                        m, j = g // 2, g % 2
                        for hh in range(2):
                            r, at = slice(hh * dk, hh * dk + dk), g * P
                            s = mm(banks[hh][0:CHUNK, at + CHUNK:at + P], k0[r, g, :], qgt[r, m, j, CHUNK:], start=True, stop=True)
                            if g == 3:
                                s.then_inc(score_ps[hh], 1)
                if on(a) and has_future(a):
                    pe.wait_ge(kh_done, a + 1)
                    for j in range(2):
                        for m in range(MC):
                            s = nc.tensor.transpose(banks[2][:, j * DK + m * P:j * DK + (m + 1) * P], kht_in[:, m, j, :], ident[:, :])
                    s.then_inc(kht_ps, 1)
                if on(p):
                    pe.wait_ge(xnT_done, p + 1)
                    count_past(pe, x2_done[1], a)
                    split("w1", p)
                    for k in range(KC):
                        for x in range(2):
                            s = mm(banks[6][:, 0:TOK], w1_s[:, k, :, :, :].rearrange("p b a r -> p (b a r)"), xnT[x][:, k, :],
                                   start=(k == x == 0), stop=(k == x == 1))
                    s.then_inc(low_ps, 1)
                if on(f):
                    pe.wait_ge(x2n_done, f + 1)
                    for k in range(KC):
                        for j in range(2):
                            s = nc.tensor.transpose(banks[3][:, k * TOK + j * P:k * TOK + (j + 1) * P], x2n[:, j, k * P:(k + 1) * P], ident[:, :])
                    s.then_inc(x2nT_ps, 1)
                if on(a):
                    pe.wait_ge(v_done[0], a + 1)
                    pe.wait_ge(v_done[1], a + 1)
                    for hh in range(2):
                        pe.wait_ge(probs_done[hh], a + 1)
                        for g in range(4):
                            m, j = g // 2, g % 2
                            h = 2 * m + hh
                            o = mm(banks[hh][:, g * dv:(g + 1) * dv], probs[:, hh, g, :], vals[:, j, h * dv:(h + 1) * dv],
                                   start=(g == 0), stop=not has_past(a), skip_group_check=True)
                        if not has_past(a):
                            o.then_inc(o_ps[hh], 1)
                if on(p):
                    pe.wait_ge(low_done, p + 1)
                    if on(f):
                        pe.wait_ge(x2nT_done, f + 1)
                    split("w2", p)
                    for m in range(MC):
                        s = mm(banks[3][:, m * TOK:(m + 1) * TOK], w2_s[:, m * P:(m + 1) * P], lowT[:, :], start=True, stop=True)
                    s.then_inc(z_ps, 1)
                if on(f):
                    pe.wait_ge(x2nT_done, f + 1)
                    count_past(pe, res_done, f)
                    split("u1", f)
                    for k in range(KC):
                        s = mm3(banks[4][:, 0:TOK], [u[:, k, :, :].rearrange("p a r -> p (a r)") for u in u1_p], both(x2nT, ALL, k), k == 0, k == KC - 1)
                    s.then_inc(pT_ps, 1)
                if on(a) and has_past(a):
                    pe.wait_ge(qs0_done, a + 1)
                    pe.wait_ge(qs1_done, a + 1)
                    for g in range(4):
                        m, j = g // 2, g % 2
                        for hh in range(2):
                            r = slice(hh * dk, hh * dk + dk)
                            s = mm(banks[hh][:, g * dv:(g + 1) * dv], qst[r, m, j, :], state[c][r, m, j, :],
                                   start=False, stop=True, skip_group_check=True)
                            if g == 3:
                                s.then_inc(o_ps[hh], 1)
                if on(a) and has_future(a):
                    pe.wait_ge(kht_done, a + 1)
                    for m in range(MC):
                        for j in range(2):
                            for hh in range(2):
                                h = 2 * m + hh
                                s = mm(banks[2][hh * dk:(hh + 1) * dk, (m * 2 + j) * dv:(m * 2 + j + 1) * dv],
                                       kht[:, j, h * dk:(h + 1) * dk], vals[:, j, h * dv:(h + 1) * dv], start=True, stop=True)
                    s.then_inc(state_ps, 1)
                if on(f):
                    pe.wait_ge(pT_done, f + 1)
                    split("v1", f)
                    for b in range(4):
                        if b == 3:
                            count_past(pe, yT_done[1], a)
                        for k in range(2):
                            fc = 2 * b + k
                            for x in range(2):
                                s = mm(banks[4 + b][:, k * TOK:(k + 1) * TOK], v1_p[x][:, fc * P:(fc + 1) * P], pT[:, :], start=(x == 0), stop=(x == 1))
                        s.then_inc(h_ps[b], 1)
                if on(p):
                    def project_v():
                        split("wv", p)
                        for j in v_order(p):
                            if j == 0:
                                if has_future(a):
                                    count_past(pe, state_done, a + 1)
                            else:
                                pe.wait_ge(minz_done, p + 1)
                            for k in range(KC):
                                s = mm3(banks[2 + j][:, :], both(xnT, ALL, k, slice(j * P, j * P + P)), both(wv_p, ALL, k), k == 0, k == KC - 1)
                            s.then_inc(v_ps[j], 1)

                    def project_qk():
                        for b, w, done in ((0, wq_p, q_ps), (1, wk_p, k_ps)):
                            split("wq" if b == 0 else "wk", p)
                            if on(f):
                                pe.wait_ge(gelu_done[b], f + 1)
                            for m in range(MC):
                                for k in range(KC):
                                    s = mm3(banks[4 + b][:, m * TOK:(m + 1) * TOK], both(w, ALL, k, slice(m * P, m * P + P)), both(xnT, ALL, k), k == 0, k == KC - 1)
                            s.then_inc(done, 1)

                    for project in (project_qk, project_v) if isinstance(p, int) and p == 1 else (project_v, project_qk):
                        project()
                if on(a):
                    pe.wait_ge(y_done[0], a + 1)
                    pe.wait_ge(y_done[1], a + 1)
                    for j in range(2):
                        if on(f):
                            pe.wait_ge(gelu_done[2 + j], f + 1)
                        for h in range(HEADS):
                            s = nc.tensor.transpose(banks[6 + j][:, h * P:(h + 1) * P], y[:, j, h * dv:(h + 1) * dv], ident[:, :])
                        s.then_inc(yT_ps[j], 1)
                if on(p):
                    split("wg", p)
                    for j in range(2):
                        for k in range(KC):
                            s = mm3(banks[j][:, :], both(xnT, ALL, k, slice(j * P, j * P + P)), both(wg_p, ALL, k), k == 0, k == KC - 1)
                        s.then_inc(g_ps[j], 1)
                if on(f):
                    if on(p):
                        pe.wait_ge(v_done[0], p + 1)
                    split("u2", f)
                    for b in range(4):
                        pe.wait_ge(h_lo[b], f + 1)
                        for fc in (2 * b, 2 * b + 1):
                            for x in range(2):
                                s = mm(banks[2][:, 0:TOK], u2_s[:, fc, :, :].rearrange("p a r -> p (a r)"), hT_p[x][:, fc, :],
                                       start=(fc == x == 0), stop=(fc == FC - 1 and x == 1))
                    s.then_inc(qT_ps, 1)
                if on(a):
                    if on(p):
                        pe.wait_ge(v_done[1], p + 1)
                    for j in range(2):
                        pe.wait_ge(yT_done[j], a + 1)
                        split("wo", a)
                        for h in range(HEADS):
                            s = mm3(banks[3 + 3 * j][:, 0:D], both(yT, ALL, j, h), both(wo_p, ALL, h), h == 0, h == HEADS - 1)
                        s.then_inc(proj_ps[j], 1)
                if on(f):
                    if on(p):
                        pe.wait_ge(qg_done, p + 1)
                    pe.wait_ge(qT_done, f + 1)
                    split("v2", f)
                    for j in range(2):
                        s = mm3(banks[4][:, j * D:(j + 1) * D], both(qT, ALL, slice(j * P, j * P + P)), both(v2_p, ALL, ALL))
                    s.then_inc(ff_ps, 1)

            run(pe, slot)


_INS = ['L0_attn_x', 'L0_attn_Wq', 'L0_attn_Wk', 'L0_attn_Wv', 'L0_attn_Wg', 'L0_attn_gk_w1', 'L0_attn_gk_w2', 'L0_attn_gk_b2',
        'L0_attn_g_norm_w', 'L0_attn_Wo', 'L0_ffn_U1', 'L0_ffn_V1', 'L0_ffn_b1', 'L0_ffn_U2', 'L0_ffn_V2', 'L0_ffn_b2']

_COLUMNS = ['L0_attn_gk_b2', 'L0_ffn_b1']


def kernel(**inputs):
    import numpy as _np
    import concourse.bacc as _bacc
    from concourse import mybir as _mybir
    from concourse.bass_utils import run_bass_kernel_spmd as _run

    nc = _bacc.Bacc("TRN2", target_bir_lowering=False, num_devices=1)
    arrays, args = {}, []
    for name in _INS:
        a = _np.asarray(inputs[name])
        if name in _COLUMNS:
            a = a.reshape(-1, P).T
        a = _np.ascontiguousarray(a)
        arrays[f"in_{name}_dram"] = a
        args.append(nc.dram_tensor(f"in_{name}_dram", a.shape, _mybir.dt.from_np(a.dtype), kind="ExternalInput").ap())
    args.append(nc.dram_tensor("out_dram", inputs['L0_attn_x'].shape, _mybir.dt.float32, kind="ExternalOutput").ap())
    build(nc, *args)
    r = _run(nc, [arrays], core_ids=[0])
    return r.results[0]["out_dram"]
```
